# Optimizing a Trainium2 kernel written in Bass

```python
import numpy as np
import jax
import jax.numpy as jnp

def _softmax(x, axis=-1):
    return jax.nn.softmax(x, axis=axis)

def _gelu(x):
    return jax.nn.gelu(x, approximate=True)

def _silu(x):
    return jax.nn.silu(x)

def _sigmoid(x):
    return jax.nn.sigmoid(x)

def _layernorm(x, axis=-1, eps=1e-05):
    m = jnp.mean(x, axis=axis, keepdims=True)
    v = jnp.var(x, axis=axis, keepdims=True)
    return (x - m) / jnp.sqrt(v + eps)

def _scatter_add(tgt, idx, src, axis=0):
    return tgt.at[idx].add(src)

def _segment_sum(src, seg, n):
    return jax.ops.segment_sum(src, seg, n)
kernel_name = 'mk_macaron_d1_jaxref_r8_ecfd3b'

def setup_inputs(seed: int=0):
    np.random.seed(seed)
    _w = jnp.asarray

    def _L0_attn_setup():
        import jax, jax.numpy as jnp
        import numpy as np
        B, T, HID = (4, 256, 128)
        H, D, V = (8, 64, 128)
        EPS = 1e-05

        def _rotary(x, T, D):
            inv_freq = 1.0 / 10000.0 ** (jnp.arange(0, D, 2, dtype=jnp.float32) / D)
            t = jnp.arange(T, dtype=jnp.float32)
            freqs = t[:, None] * inv_freq[None, :]
            emb = jnp.concatenate([freqs, freqs], axis=-1)
            cos = jnp.cos(emb)[None, None, :, :]
            sin = jnp.sin(emb)[None, None, :, :]
            x1, x2 = jnp.split(x, 2, axis=-1)
            rot = jnp.concatenate([-x2, x1], axis=-1)
            return x * cos + rot * sin
        key = jax.random.key(seed)
        ks = jax.random.split(key, 7)
        sc = 0.02
        return {'x': jax.random.normal(ks[0], (B, T, HID), dtype=jnp.float32), 'Wq': jax.random.normal(ks[1], (H * D, HID), dtype=jnp.float32) * sc, 'Wk': jax.random.normal(ks[2], (H * D, HID), dtype=jnp.float32) * sc, 'Wv': jax.random.normal(ks[3], (H * V, HID), dtype=jnp.float32) * sc, 'Wg': jax.random.normal(ks[4], (H * V, HID), dtype=jnp.float32) * sc, 'Wo': jax.random.normal(ks[5], (HID, H * V), dtype=jnp.float32) * sc, 'gn_weight': jnp.ones((H * V,), dtype=jnp.float32), 'gn_bias': jnp.zeros((H * V,), dtype=jnp.float32)}
    _L0_attn_in = _L0_attn_setup()

    def _L0_ffn_setup():
        import jax, jax.numpy as jnp
        import numpy as np
        D = 128
        H = 16
        DK = D // H
        E = 8
        DFF = 4 * D
        TOPK = 2
        EPS = 1e-05

        def _layernorm(x, g, b):
            m = jnp.mean(x, axis=-1, keepdims=True)
            v = jnp.mean(jnp.square(x - m), axis=-1, keepdims=True)
            return (x - m) * jax.lax.rsqrt(v + EPS) * g + b
        key = jax.random.key(seed)
        ks = jax.random.split(key, 16)
        s_in = 1.0 / np.sqrt(D)
        s_ff = 1.0 / np.sqrt(DFF)
        return {'x': jax.random.normal(ks[0], (2, 256, D), dtype=jnp.float32), 'ln1_g': jnp.ones((D,), jnp.float32), 'ln1_b': jnp.zeros((D,), jnp.float32), 'w_qkv': jax.random.normal(ks[1], (D, 3 * D), jnp.float32) * s_in, 'b_qkv': jnp.zeros((3 * D,), jnp.float32), 'w_o': jax.random.normal(ks[2], (D, D), jnp.float32) * s_in, 'b_o': jnp.zeros((D,), jnp.float32), 'ln2_g': jnp.ones((D,), jnp.float32), 'ln2_b': jnp.zeros((D,), jnp.float32), 'gate_w': jax.random.normal(ks[3], (D, E), jnp.float32) * s_in, 'gate_b': jnp.zeros((E,), jnp.float32), 'W1': jax.random.normal(ks[4], (E, D, DFF), jnp.float32) * s_in, 'b1': jnp.zeros((E, DFF), jnp.float32), 'W2': jax.random.normal(ks[5], (E, DFF, D), jnp.float32) * s_ff, 'b2': jnp.zeros((E, D), jnp.float32)}
    _L0_ffn_in = _L0_ffn_setup()
    _d = {'L0_attn_x': _L0_attn_in['x'], 'L0_attn_Wq': _L0_attn_in['Wq'], 'L0_attn_Wk': _L0_attn_in['Wk'], 'L0_attn_Wv': _L0_attn_in['Wv'], 'L0_attn_Wg': _L0_attn_in['Wg'], 'L0_attn_Wo': _L0_attn_in['Wo'], 'L0_attn_gn_weight': _L0_attn_in['gn_weight'], 'L0_attn_gn_bias': _L0_attn_in['gn_bias'], 'L0_ffn_ln1_g': _L0_ffn_in['ln1_g'], 'L0_ffn_ln1_b': _L0_ffn_in['ln1_b'], 'L0_ffn_w_qkv': _L0_ffn_in['w_qkv'], 'L0_ffn_b_qkv': _L0_ffn_in['b_qkv'], 'L0_ffn_w_o': _L0_ffn_in['w_o'], 'L0_ffn_b_o': _L0_ffn_in['b_o'], 'L0_ffn_ln2_g': _L0_ffn_in['ln2_g'], 'L0_ffn_ln2_b': _L0_ffn_in['ln2_b'], 'L0_ffn_gate_w': _L0_ffn_in['gate_w'], 'L0_ffn_gate_b': _L0_ffn_in['gate_b'], 'L0_ffn_W1': _L0_ffn_in['W1'], 'L0_ffn_b1': _L0_ffn_in['b1'], 'L0_ffn_W2': _L0_ffn_in['W2'], 'L0_ffn_b2': _L0_ffn_in['b2']}
    _x0 = _d['L0_attn_x']
    _d['L0_attn_x'] = jax.random.normal(jax.random.fold_in(jax.random.key(seed), 1), (8, 256, 128), dtype=_x0.dtype)
    del _x0
    return _d

def reference(L0_attn_x, L0_attn_Wq, L0_attn_Wk, L0_attn_Wv, L0_attn_Wg, L0_attn_Wo, L0_attn_gn_weight, L0_attn_gn_bias, L0_ffn_ln1_g, L0_ffn_ln1_b, L0_ffn_w_qkv, L0_ffn_b_qkv, L0_ffn_w_o, L0_ffn_b_o, L0_ffn_ln2_g, L0_ffn_ln2_b, L0_ffn_gate_w, L0_ffn_gate_b, L0_ffn_W1, L0_ffn_b1, L0_ffn_W2, L0_ffn_b2):

    def _L0_attn_ref(x, Wq, Wk, Wv, Wg, Wo, gn_weight, gn_bias):
        import jax, jax.numpy as jnp
        import numpy as np
        B, T, HID = (4, 256, 128)
        H, D, V = (8, 64, 128)
        EPS = 1e-05

        def _rotary(x, T, D):
            inv_freq = 1.0 / 10000.0 ** (jnp.arange(0, D, 2, dtype=jnp.float32) / D)
            t = jnp.arange(T, dtype=jnp.float32)
            freqs = t[:, None] * inv_freq[None, :]
            emb = jnp.concatenate([freqs, freqs], axis=-1)
            cos = jnp.cos(emb)[None, None, :, :]
            sin = jnp.sin(emb)[None, None, :, :]
            x1, x2 = jnp.split(x, 2, axis=-1)
            rot = jnp.concatenate([-x2, x1], axis=-1)
            return x * cos + rot * sin
        Bx, Tx, _ = x.shape
        q = jnp.einsum('bti,oi->bto', x, Wq).reshape(Bx, Tx, H, D).transpose(0, 2, 1, 3)
        k = jnp.einsum('bti,oi->bto', x, Wk).reshape(Bx, Tx, H, D).transpose(0, 2, 1, 3)
        v = jnp.einsum('bti,oi->bto', x, Wv).reshape(Bx, Tx, H, V).transpose(0, 2, 1, 3)
        g = jnp.einsum('bti,oi->bto', x, Wg)
        q = _rotary(q, Tx, D)
        k = _rotary(k, Tx, D)
        gamma = 1.0 - jnp.exp2(-5.0 - jnp.arange(H, dtype=jnp.float32))
        s = jnp.log2(gamma)
        n = jnp.arange(Tx, dtype=jnp.float32)
        rel = n[:, None] - n[None, :]
        causal = rel >= 0
        decay = jnp.where(causal[None, :, :], jnp.exp2(rel[None, :, :] * s[:, None, None]), 0.0)
        scores = jnp.einsum('bhtd,bhsd->bhts', q, k) * D ** (-0.5)
        scores = scores * decay[None]
        o = jnp.einsum('bhts,bhsv->bhtv', scores, v)
        o = o.transpose(0, 2, 1, 3)
        mean = jnp.mean(o, axis=-1, keepdims=True)
        var = jnp.var(o, axis=-1, keepdims=True)
        o = (o - mean) * jax.lax.rsqrt(var + EPS)
        o = o * gn_weight.reshape(H, V) + gn_bias.reshape(H, V)
        o = o.reshape(Bx, Tx, H * V)
        o = o * jax.nn.silu(g)
        return jnp.einsum('btc,oc->bto', o, Wo)

    def _L0_ffn_ref(x, ln1_g, ln1_b, w_qkv, b_qkv, w_o, b_o, ln2_g, ln2_b, gate_w, gate_b, W1, b1, W2, b2):
        import jax, jax.numpy as jnp
        import numpy as np
        D = 128
        H = 16
        DK = D // H
        E = 8
        DFF = 4 * D
        TOPK = 2
        EPS = 1e-05

        def _layernorm(x, g, b):
            m = jnp.mean(x, axis=-1, keepdims=True)
            v = jnp.mean(jnp.square(x - m), axis=-1, keepdims=True)
            return (x - m) * jax.lax.rsqrt(v + EPS) * g + b
        B, S, _ = x.shape
        h = _layernorm(x, ln1_g, ln1_b)
        qkv = h @ w_qkv + b_qkv
        q, k, v = jnp.split(qkv, 3, axis=-1)
        q = q.reshape(B, S, H, DK)
        k = k.reshape(B, S, H, DK)
        v = v.reshape(B, S, H, DK)
        scores = jnp.einsum('bqhd,bkhd->bhqk', q, k) / np.sqrt(DK)
        attn = jax.nn.softmax(scores, axis=-1)
        o = jnp.einsum('bhqk,bkhd->bqhd', attn, v).reshape(B, S, D)
        x = x + o @ w_o + b_o
        h = _layernorm(x, ln2_g, ln2_b).reshape(B * S, D)
        logits = h @ gate_w + gate_b
        topv, topi = jax.lax.top_k(logits, TOPK)
        gw = jax.nn.softmax(topv, axis=-1)
        ew = jnp.sum(jax.nn.one_hot(topi, E, dtype=h.dtype) * gw[..., None], axis=1)
        hid = jax.nn.relu(jnp.einsum('td,edf->etf', h, W1) + b1[:, None, :])
        out_e = jnp.einsum('etf,efd->etd', hid, W2) + b2[:, None, :]
        moe = jnp.einsum('etd,te->td', out_e, ew)
        return x + moe.reshape(B, S, D)
    x = L0_attn_x
    x = x + 0.5 * _L0_ffn_ref(_layernorm(x, axis=-1), L0_ffn_ln1_g, L0_ffn_ln1_b, L0_ffn_w_qkv, L0_ffn_b_qkv, L0_ffn_w_o, L0_ffn_b_o, L0_ffn_ln2_g, L0_ffn_ln2_b, L0_ffn_gate_w, L0_ffn_gate_b, L0_ffn_W1, L0_ffn_b1, L0_ffn_W2, L0_ffn_b2)
    x = x + _L0_attn_ref(_layernorm(x, axis=-1), L0_attn_Wq, L0_attn_Wk, L0_attn_Wv, L0_attn_Wg, L0_attn_Wo, L0_attn_gn_weight, L0_attn_gn_bias)
    x = x + 0.5 * _L0_ffn_ref(_layernorm(x, axis=-1), L0_ffn_ln1_g, L0_ffn_ln1_b, L0_ffn_w_qkv, L0_ffn_b_qkv, L0_ffn_w_o, L0_ffn_b_o, L0_ffn_ln2_g, L0_ffn_ln2_b, L0_ffn_gate_w, L0_ffn_gate_b, L0_ffn_W1, L0_ffn_b1, L0_ffn_W2, L0_ffn_b2)
    return x

_drawn_inputs = setup_inputs


def setup_inputs(seed=0):
    import zlib

    import numpy as np

    out = dict(_drawn_inputs(seed))
    spreads = {'L0_attn_gn_weight': (1.0, 0.6),
     'L0_attn_gn_bias': (0.0, 0.8),
     'L0_ffn_ln1_g': (1.0, 0.2),
     'L0_ffn_ln1_b': (0.0, 0.1),
     'L0_ffn_b_qkv': (0.0, 0.1),
     'L0_ffn_b_o': (0.0, 0.1),
     'L0_ffn_ln2_g': (1.0, 0.2),
     'L0_ffn_ln2_b': (0.0, 0.1),
     'L0_ffn_gate_b': (0.0, 0.1),
     'L0_ffn_b1': (0.0, 0.1),
     'L0_ffn_b2': (0.0, 0.1)}
    factors = {}
    for name, (base, spread) in spreads.items():
        noise = np.random.default_rng([zlib.crc32(name.encode()), seed]).standard_normal(out[name].shape)
        drawn = base * np.exp(spread * noise) if base else spread * noise
        out[name] = jnp.asarray(drawn.astype(out[name].dtype))
    for name, factor in factors.items():
        out[name] = (out[name] * factor).astype(out[name].dtype)
    return out
```

```python
from contextlib import ExitStack

import numpy as np
import concourse.bass as bass
from concourse import mybir

F32 = mybir.dt.float32
F32R = mybir.dt.float32r
U32 = mybir.dt.uint32
ALU = mybir.AluOpType
ACT = mybir.ActivationFunctionType
AX = mybir.AxisListType

P = 128
SEQ = 256
D = 128
CT = 4
CH = CT * P
CB = CH // SEQ
EPS = 1e-5
HA, DK = 16, 8
GA = 4
E, FT = 8, 4
HR, DR = 8, 64
AUG = 24


class Signal:

    def __init__(self, sem, per):
        self.sem, self.per = sem, per

    def __call__(self, n, k):
        return n * self.per + k


def constants(NT):
    inv = (1.0 / np.float32(10000.0) ** (np.arange(0, DR, 2, dtype=np.float32) / np.float32(DR))).astype(np.float32)
    fr = np.arange(SEQ, dtype=np.float32)[:, None] * inv[None, :]
    emb = np.concatenate([fr, fr], -1)
    cos = np.tile(np.cos(emb).T, (2, 1)).astype(np.float32)
    sin = np.tile(np.sin(emb).T, (2, 1)).astype(np.float32)
    gamma = 1.0 - np.exp2(-5.0 - np.arange(HR, dtype=np.float64))
    s = np.arange(P)[:, None]
    dec = np.zeros((P, HR, 3 * P))
    for h in range(HR):
        rel = np.arange(P)[None, :] - s
        diag = np.where(rel >= 0, gamma[h] ** np.maximum(rel, 0), 0.0)
        dec[:, h, 0:P] = diag
        dec[:, h, P:2 * P] = gamma[h] ** (rel + P)
        dec[:, h, 2 * P:] = diag
    dec *= DR ** -0.5
    sel = np.zeros((E, E, P), np.float32)
    for e in range(E):
        sel[e, e, :] = 1.0
    mask = np.zeros((P, 2), np.float32)
    for j in range(4):
        mask[32 * j + 16:32 * j + 24, 0] = -1.0
        mask[32 * j + 8:32 * j + 16, 1] = -1.0
    return {
        "c_ident": np.eye(P, dtype=np.float32), "c_cos": cos, "c_sin": sin,
        "c_decay": dec.astype(np.float32).reshape(P, HR * 3 * P), "c_sel": sel.reshape(E, E * P),
        "c_iota": np.tile(np.arange(E, dtype=np.float32), (P, 1)), "c_mask": mask,
    }


def build(nc, a, out):
    x_d = a["L0_attn_x"]
    NTOK = x_d.shape[0] * x_d.shape[1]
    NT = NTOK // P
    NCH = NTOK // CH
    ctx = ExitStack()
    scope = [ctx]
    with ctx:
        def sb(name, shape, dt=F32):
            return scope[0].enter_context(nc.sbuf_tensor(name, shape, dt))

        def sg(name, per):
            return Signal(ctx.enter_context(nc.semaphore(name)), per)

        x_sb = sb("x_sb", [P, NT, D])
        w1 = sb("w1", [P, E, FT * P])
        w2 = sb("w2", [P, E, FT, D])
        wqkv = sb("wqkv", [P, 3 * D])
        wqp = sb("wqp", [P, GA, 4, 4, DK])
        wkp = sb("wkp", [P, GA, 4, 4, DK])
        wo = sb("wo", [P, D])
        gate_w = sb("gate_w", [P, E])
        b2 = sb("b2", [E, D])
        bqkv = sb("bqkv", [1, 3 * D])
        bqp = sb("bqp", [1, 2, GA, 4, 4, DK])
        one1 = sb("one1", [1, 1])
        bqk = sb("bqk", [P, 2, GA])
        bv_bc = sb("bv_bc", [P, D])
        bo_bc = sb("bo_bc", [P, D])
        gb_bc = sb("gb_bc", [P, E])
        vec_rows = sb("vec_rows", [52, P])
        vec = sb("vec", [P, 52])
        ident = sb("ident", [P, P])
        cos = sb("cos", [P, SEQ])
        sin = sb("sin", [P, SEQ])
        decay = sb("decay", [P, HR, 3 * P])
        sel = sb("sel", [E, E, P])
        iota = sb("iota", [P, E])
        mask = sb("mask", [P, 2])
        ret_in = sb("ret_in", [P, 24, P])
        wo_in = sb("wo_in", [P, HR * P])
        rw = sb("rw", [P, 24, P])
        rrot = sb("rrot", [P, 8, P])
        rwo = sb("rwo", [P, HR, D])
        mhalf = sb("mhalf", [P, CT])
        B1, GNW, GNB, G1, L1B, G2, L2B = 0, 32, 40, 48, 49, 50, 51

        vaug = sb("vaug", [P, CT, HA, 32])
        msp = sb("msp", [P, 2, 2, P])
        ln_t = sb("ln_t", [P, 6, CT])
        st = sb("st", [P, CT, 6])
        mv = sb("mv", [P, CT, 2])
        r1 = sb("r1", [P, CT])
        r12 = sb("r12", [P, CT])
        z = sb("z", [P, CT, D])
        ffn_only = ExitStack()
        scope[0] = ffn_only
        xn = sb("xn", [P, CT, D])
        hT = sb("hT", [P, CH])
        tqk = sb("tqk", [P, 2, CH])
        hi = sb("hi", [P, 2, CH], F32R)
        qp = sb("qp", [P, GA, CH], F32R)
        kp = sb("kp", [P, GA, CH], F32R)
        qm = sb("qm", [P, 2, SEQ], F32R)
        pt = sb("pt", [P, 2, 2, 2 * SEQ])
        ou = sb("ou", [P, 2, SEQ])
        rec = sb("rec", [P, 2, 2, 4])
        o_tm = sb("o_tm", [P, CT, D])
        oT = sb("oT", [P, CH])
        x1 = sb("x1", [P, CT, D])
        st2 = sb("st2", [P, CT, 6])
        mv2 = sb("mv2", [P, CT, 2])
        r2 = sb("r2", [P, CT])
        z2 = sb("z2", [P, CT, D])
        h2T = sb("h2T", [P, CH])
        lg = sb("lg", [P, CT, E])
        top = sb("top", [P, CT, 8])
        tix = sb("tix", [P, CT, 8], U32)
        tif = sb("tif", [P, CT, 2])
        dv = sb("dv", [P, CT])
        ev = sb("ev", [P, CT])
        den = sb("den", [P, CT])
        gw1 = sb("gw1", [P, CT])
        gw2 = sb("gw2", [P, CT])
        ew_a = sb("ew_a", [P, CT, E])
        ew_b = sb("ew_b", [P, CT, E])
        ew = sb("ew", [P, CT, E])
        ewT = sb("ewT", [E, CH])
        ewb = sb("ewb", [P, 2, CH])
        hid = sb("hid", [P, 2, FT, CH])
        tmp = sb("tmp", [P, 2, CH])
        acc = sb("acc", [P, CH])
        ffn_only.close()
        scope[0] = ctx
        zT = sb("zT", [P, CH])
        ra = sb("ra", [P, 2, CH])
        rb = sb("rb", [P, 2, CH])
        qr = sb("qr", [P, 4, CH])
        kr = sb("kr", [P, 4, CH])
        vr = sb("vr", [P, CT, HR * P])
        th = sb("th", [P, 2, CH])
        sgT = sb("sgT", [P, HR, CH])
        sc = sb("sc", [P, 2, 3 * P])
        ost = sb("ost", [P, 2, 2, 6])
        omv = sb("omv", [P, 2, 2, 2])
        ors = sb("ors", [P, 2, 4, 2])
        oh = sb("oh", [P, 2, 2, P])
        on = sb("on", [P, 2, SEQ])
        yT = sb("yT", [P, HR, CH])

        ps = ctx.enter_context(nc.psum_tensor("ps", [P, 8, 512], F32))

        ld = {k: ctx.enter_context(nc.semaphore("ld_" + k)) for k in ("x", "w", "r", "moe")}
        zeroed = sg("zeroed", 0)
        spread = sg("spread", 0)
        vec_ps = sg("vec_ps", 0)
        vec_sb = sg("vec_sb", 0)
        rw_ps = sg("rw_ps", 0)
        rw_sb = sg("rw_sb", 0)
        rot_w = sg("rot_w", 0)
        f = {k: sg("f_" + k, v) for k, v in dict(
            stat=8, rstd=1, xn=4, z=4, xnb=1, hTp=1, hT=1, qkp=8, tqk=8, hi=8, pack=8, vps=1, vaug=1,
            s_ps=16, smax=16, mTp=8, qm=8, st_ps=16, pexp=16, pv=16, ou=8, oqp=8, rec=8, o_tm=8, oTp=1, oT=1,
            x1p=1, x1=1, stat2=8, rstd2=1, z2=4, h2Tp=1, h2T=1, lgp=1, lg=1, top=4, tix=4, dv=2, ev=1, gw=3, ewab=8,
            ew=1, ewTp=1, ewT=1, zps=32, hid=32, ewbp=8, ewb=8, b2p=1, outp=8, tmp=8, acc0=1, acc=8, accTp=1,
            y=1, x_done=1, chain=7).items()}
        r = {k: sg("r_" + k, v) for k, v in dict(
            stat=8, rstd=1, z=4, zTp=1, zT=1, qkp=16, rab=16, rot=8, vp=8, vr=8, gp=8, th=8, sgT=8,
            scp=16, sc=16, op=16, ost=32, omv=32, ors=16, oh=32, ohTp=16, on=16, yT=16, wop=1, x_done=1,
            chain=1 + 16 * 3).items()}
        stored = ctx.enter_context(nc.semaphore("stored"))
        passed = ctx.enter_context(nc.semaphore("passed"))
        x_flat = x_sb[:].rearrange("p n d -> p (n d)")
        x_tok = x_d.rearrange("b (t p) d -> p (b t) d", p=P)
        out_tok = out.rearrange("b (t p) d -> p (b t) d", p=P)
        NLD_W, NLD_MOE, NLD_R = 17, 4, 8

        block = ctx.enter_context(nc.Block())

        def wait(e, sig, n, k):
            e.wait_ge(sig.sem, sig(n, k))

        def wait_alone(e, sig, n, k):
            e.wait_ge(sig.sem, sig(n, k))
            e.sem_inc(passed)

        @block.sync
        def _(e):
            e.dma_start(x_sb[:], x_tok).then_inc(ld["x"], 16)
            for dst, src in (
                (ident[:], a["c_ident"]), (wqkv[:], a["L0_ffn_w_qkv"]),
                (bqkv[:], a["L0_ffn_b_qkv"].unsqueeze(0)),
                (vec_rows[B1:B1 + 32, :], a["L0_ffn_b1"].rearrange("e (k f) -> (e k) f", f=P)),
                (vec_rows[GNW:GNW + 8, :], a["L0_attn_gn_weight"].rearrange("(h f) -> h f", f=P)),
                (vec_rows[GNB:GNB + 8, :], a["L0_attn_gn_bias"].rearrange("(h f) -> h f", f=P)),
                (vec_rows[G1:G1 + 1, :], a["L0_ffn_ln1_g"].unsqueeze(0)),
                (vec_rows[L1B:L1B + 1, :], a["L0_ffn_ln1_b"].unsqueeze(0)),
                (vec_rows[G2:G2 + 1, :], a["L0_ffn_ln2_g"].unsqueeze(0)),
                (vec_rows[L2B:L2B + 1, :], a["L0_ffn_ln2_b"].unsqueeze(0)),
                (mask[:], a["c_mask"]), (iota[:], a["c_iota"]),
                (bv_bc[:], a["L0_ffn_b_qkv"][2 * D:3 * D].partition_broadcast(P)),
                (bo_bc[:], a["L0_ffn_b_o"].partition_broadcast(P)),
                (gb_bc[:], a["L0_ffn_gate_b"].partition_broadcast(P)),
                (wo[:], a["L0_ffn_w_o"]), (gate_w[:], a["L0_ffn_gate_w"]),
            ):
                e.dma_start(dst, src).then_inc(ld["w"], 16)
            e.dma_start(w1[:], a["L0_ffn_W1"].rearrange("e d f -> d e f")).then_inc(ld["moe"], 16)
            e.dma_start(w2[:], a["L0_ffn_W2"].rearrange("e (k f) d -> f e k d", f=P)).then_inc(ld["moe"], 16)
            e.dma_start(b2[:], a["L0_ffn_b2"]).then_inc(ld["moe"], 16)
            e.dma_start(sel[:], a["c_sel"].rearrange("e (k f) -> e k f", f=P)).then_inc(ld["moe"], 16)
            for name, at in (("Wq", 0), ("Wk", 4), ("Wv", 8), ("Wg", 16)):
                w = a["L0_attn_" + name].rearrange("(k o) i -> o k i", o=P)
                e.dma_start(ret_in[:, at:at + w.shape[1], :], w).then_inc(ld["r"], 16)
            e.dma_start(wo_in[:], a["L0_attn_Wo"]).then_inc(ld["r"], 16)
            e.dma_start(decay[:], a["c_decay"].rearrange("p (h k) -> p h k", h=HR)).then_inc(ld["r"], 16)
            e.dma_start(cos[:], a["c_cos"]).then_inc(ld["r"], 16)
            e.dma_start(sin[:], a["c_sin"]).then_inc(ld["r"], 16)
            with e.Fori(0, NCH) as c:
                wait(e, f["x_done"], c + NCH, 1)
                e.dma_start(out_tok[:, bass.ds(c * CT, CT), :], x_sb[:, bass.ds(c * CT, CT), :]).then_inc(stored, 16)
            e.wait_ge(stored, 16 * NCH)

        def rsqrt_chain(e, steps, chain, n, k0, last):
            for i, ins in enumerate(steps):
                if i:
                    wait_alone(e, chain, n, k0 + i)
                done = ins()
                if i + 1 < len(steps):
                    done.then_inc(chain.sem, 1)
            done.then_inc(last.sem, 1)

        def pool_tt(e, o, a0, a1, op):
            return lambda: e.tensor_tensor(o, a0, a1, op)

        def pool_ve(e, o, v):
            return lambda: e.tensor_scalar(o, v, 1.0, EPS, ALU.mult, ALU.add)

        def pool_ffn(e, n):
            wait_alone(e, f["stat"], n, 8)
            rsqrt_chain(e, [
                pool_ve(e, ln_t[:, 0, :], mv[:, :, 1]),
                pool_tt(e, r1[:], ln_t[:, 0, :], mhalf[:], ALU.pow),
                pool_tt(e, ln_t[:, 1, :], r1[:], r1[:], ALU.mult),
                pool_tt(e, ln_t[:, 2, :], ln_t[:, 1, :], mv[:, :, 1], ALU.mult),
                pool_ve(e, ln_t[:, 3, :], ln_t[:, 2, :]),
                pool_tt(e, ln_t[:, 4, :], ln_t[:, 3, :], mhalf[:], ALU.pow),
                pool_tt(e, r12[:], r1[:], ln_t[:, 4, :], ALU.mult)], f["chain"], n, 0, f["rstd"])
            wait(e, f["xn"], n, 4)
            e.tensor_tensor(xn[:], xn[:], bo_bc[:].unsqueeze(1).broadcast_to([P, CT, D]), ALU.add).then_inc(f["xnb"].sem, 1)
            for i in range(8):
                if i >= 2:
                    wait(e, f["pack"], n, i - 1)
                wait_alone(e, f["tqk"], n, i + 1)
                e.tensor_copy(hi[:, i % 2, :], tqk[:, i % 2, :]).then_inc(f["hi"].sem, 1)
            wait_alone(e, f["stat2"], n, 8)
            rsqrt_chain(e, [
                pool_ve(e, ln_t[:, 5, :], mv2[:, :, 1]),
                pool_tt(e, r2[:], ln_t[:, 5, :], mhalf[:], ALU.pow)], f["chain"], n, 6, f["rstd2"])
            wait(e, f["acc0"], n, 1)
            for x in range(E):
                wait(e, f["tmp"], n, x + 1)
                if x:
                    wait(e, f["acc"], n, x)
                e.tensor_tensor(acc[:], acc[:], tmp[:, x % 2, :], ALU.add).then_inc(f["acc"].sem, 1)

        def pool_ret(e, n):
            wait_alone(e, r["stat"], n, 8)
            rsqrt_chain(e, [
                pool_ve(e, ln_t[:, 0, :], mv[:, :, 1]),
                pool_tt(e, r1[:], ln_t[:, 0, :], mhalf[:], ALU.pow)], r["chain"], n, 0, r["rstd"])
            for i in range(8):
                wait(e, r["rab"], n, 2 * i + 2)
                e.tensor_tensor((kr if i % 2 else qr)[:, i // 2, :], ra[:, i % 2, :], rb[:, i % 2, :], ALU.add).then_inc(r["rot"].sem, 1)

            def gated(u):
                wait(e, r["on"], n, u + 1)
                h, lo = u % HR, u // HR * SEQ
                e.tensor_tensor(yT[:, h, lo:lo + SEQ], on[:, u % 2, :], sgT[:, h, lo:lo + SEQ], ALU.mult).then_inc(r["yT"].sem, 1)

            wait(e, r["sgT"], n, 8)
            for u in range(16):
                b = u % 2
                if u >= 2:
                    wait(e, r["oh"], n, 2 * u - 2)
                wait_alone(e, r["omv"], n, 2 * u + 2)
                rsqrt_chain(e, [
                    pool_ve(e, ors[:, b, 0, :], omv[:, b, :, 1]),
                    pool_tt(e, ors[:, b, 1, :], ors[:, b, 0, :], mhalf[:, 0:2], ALU.pow),
                    lambda: e.tensor_tensor(ors[:, b, 2, :], ors[:, b, 1, :], omv[:, b, :, 0], ALU.mult),
                    lambda: e.tensor_scalar(ors[:, b, 3, :], ors[:, b, 2, :], -1.0, 1.0, ALU.mult, ALU.mult)], r["chain"], n, 1 + 3 * u, r["ors"])
                if u:
                    gated(u - 1)
            gated(15)

        @block.gpsimd
        def _(e):
            e.memset(mhalf[:], -0.5).then_inc(zeroed.sem, 1)
            e.memset(vaug[:], 0.0).then_inc(zeroed.sem, 1)
            e.memset(msp[:], 0.0).then_inc(zeroed.sem, 1)
            e.wait_ge(zeroed.sem, 3)
            e.memset(vaug[:, :, :, DK:DK + 1], 1.0).then_inc(zeroed.sem, 1)
            e.wait_ge(ld["w"], 16 * NLD_W)
            with e.Fori(0, NCH) as c:
                pool_ffn(e, c)
            with e.Fori(0, NCH) as c:
                pool_ret(e, c)
            with e.Fori(0, NCH) as c:
                pool_ffn(e, c + NCH)

        def norm_stats(e, n, src, s_, m_, sig):
            for t in range(CT):
                e.bn_stats(s_[:, t, :], src(t)).then_inc(sig.sem, 1)
            for t in range(CT):
                wait_alone(e, sig, n, t + 1)
                e.bn_aggr(m_[:, t, :], s_[:, t, :]).then_inc(sig.sem, 1)

        def dve_ffn(e, n, c):
            def x_tile(t):
                return x_flat[:, bass.ds((c * CT + t) * D, D)]

            norm_stats(e, n, x_tile, st, mv, f["stat"])
            wait(e, f["stat"], n, 8)
            wait(e, f["rstd"], n, 1)
            for t in range(CT):
                e.tensor_scalar(z[:, t, :], x_tile(t), mv[:, t, 0:1], r12[:, t:t + 1], ALU.subtract, ALU.mult).then_inc(f["z"].sem, 1)
            for t in range(CT):
                e.tensor_scalar(xn[:, t, :], x_tile(t), mv[:, t, 0:1], r1[:, t:t + 1], ALU.subtract, ALU.mult).then_inc(f["xn"].sem, 1)
            for i in range(8):
                wait(e, f["hi"], n, i + 1)
                e.scalar_tensor_tensor((kp if i % 2 else qp)[:, i // 2, :], hi[:, i % 2, :], mask[:, i % 2:i % 2 + 1], tqk[:, i % 2, :],
                                       ALU.mult, ALU.add).then_inc(f["pack"].sem, 1)
            wait(e, f["vps"], n, 1)
            e.tensor_tensor(vaug[:, :, :, 0:DK], ps[:, 4, :].rearrange("p (t h k) -> p t h k", t=CT, k=DK),
                            bv_bc[:].rearrange("p (h k) -> p h k", k=DK).unsqueeze(1).broadcast_to([P, CT, HA, DK]), ALU.add).then_inc(f["vaug"].sem, 1)

            def weigh(s):
                bb, g = divmod(s, GA)
                wait(e, f["oqp"], n, s + 1)
                o = ps[:, 7, 0:SEQ].rearrange("p (q j k) -> p q j k", q=2, k=32)
                e.reciprocal(rec[:, s % 2, :, :], o[:, :, :, DK]).then_inc(f["rec"].sem, 1)
                wait(e, f["rec"], n, s + 1)
                e.tensor_tensor(o_tm[:, 2 * bb:2 * bb + 2, 32 * g:32 * g + 32].rearrange("p q (j k) -> p q j k", k=DK), o[:, :, :, 0:DK],
                                rec[:, s % 2, :, :].unsqueeze(3).broadcast_to([P, 2, 4, DK]), ALU.mult).then_inc(f["o_tm"].sem, 1)

            for s in range(8):
                bb, g = divmod(s, GA)
                for pr in range(2):
                    wait(e, f["s_ps"], n, 2 * s + pr + 1)
                    e.tensor_reduce(msp[:, s % 2, :, 64 * pr + AUG:64 * pr + AUG + 33:32].rearrange("p q j -> p j q"),
                                    ps[:, 2 * pr:2 * pr + 2, :].rearrange("p j (q k) -> p j q k", q=2), AX.X, ALU.max, negate=True).then_inc(f["smax"].sem, 1)
                if s >= 2:
                    weigh(s - 2)
                wait(e, f["mTp"], n, s + 1)
                e.tensor_tensor(qm[:, s % 2, :], ps[:, 7, 0:SEQ], qp[:, g, bb * SEQ:(bb + 1) * SEQ].bitcast(F32), ALU.add).then_inc(f["qm"].sem, 1)
            weigh(6)
            weigh(7)
            wait(e, f["x1p"], n, 1)
            wait(e, f["xnb"], n, 1)
            e.tensor_tensor(x1[:].rearrange("p t d -> p (t d)"), ps[:, 1, :], xn[:].rearrange("p t d -> p (t d)"), ALU.add).then_inc(f["x1"].sem, 1)
            wait(e, f["x1"], n, 1)
            norm_stats(e, n, lambda t: x1[:, t, :], st2, mv2, f["stat2"])
            wait(e, f["stat2"], n, 8)
            wait(e, f["rstd2"], n, 1)
            for t in range(CT):
                e.tensor_scalar(z2[:, t, :], x1[:, t, :], mv2[:, t, 0:1], r2[:, t:t + 1], ALU.subtract, ALU.mult).then_inc(f["z2"].sem, 1)
            wait(e, f["lgp"], n, 1)
            e.tensor_tensor(lg[:], ps[:, 3, 0:CT * E].rearrange("p (t x) -> p t x", x=E), gb_bc[:].unsqueeze(1).broadcast_to([P, CT, E]), ALU.add).then_inc(f["lg"].sem, 1)
            wait_alone(e, f["lg"], n, 1)
            for t in range(CT):
                e.max(top[:, t, :], lg[:, t, :]).then_inc(f["top"].sem, 1)
            wait(e, f["top"], n, 4)
            e.tensor_tensor(dv[:], top[:, :, 1], top[:, :, 0], ALU.subtract).then_inc(f["dv"].sem, 1)
            for t in range(CT):
                e.max_index(tix[:, t, :], top[:, t, :], lg[:, t, :]).then_inc(f["tix"].sem, 1)
            wait(e, f["tix"], n, 4)
            e.tensor_copy(tif[:], tix[:, :, 0:2]).then_inc(f["dv"].sem, 1)
            wait(e, f["ev"], n, 1)
            e.tensor_scalar(den[:], ev[:], 1.0, None, ALU.add).then_inc(f["gw"].sem, 1)
            wait(e, f["gw"], n, 1)
            e.reciprocal(gw1[:], den[:]).then_inc(f["gw"].sem, 1)
            wait(e, f["gw"], n, 2)
            e.tensor_tensor(gw2[:], ev[:], gw1[:], ALU.mult).then_inc(f["gw"].sem, 1)
            wait(e, f["gw"], n, 3)
            wait(e, f["dv"], n, 2)
            for t in range(CT):
                e.tensor_scalar(ew_a[:, t, :], iota[:], tif[:, t, 0:1], gw1[:, t:t + 1], ALU.is_equal, ALU.mult).then_inc(f["ewab"].sem, 1)
                e.tensor_scalar(ew_b[:, t, :], iota[:], tif[:, t, 1:2], gw2[:, t:t + 1], ALU.is_equal, ALU.mult).then_inc(f["ewab"].sem, 1)
            wait(e, f["ewab"], n, 8)
            e.tensor_tensor(ew[:], ew_a[:], ew_b[:], ALU.add).then_inc(f["ew"].sem, 1)
            wait(e, f["b2p"], n, 1)
            e.tensor_copy(acc[:], ps[:, 6, :]).then_inc(f["acc0"].sem, 1)
            for x in range(E):
                wait(e, f["outp"], n, x + 1)
                wait(e, f["ewb"], n, x + 1)
                if x >= 2:
                    wait(e, f["acc"], n, x - 1)
                e.tensor_tensor(tmp[:, x % 2, :], ps[:, 2 + x % 2, :], ewb[:, x % 2, :], ALU.mult).then_inc(f["tmp"].sem, 1)
            wait(e, f["accTp"], n, 1)
            e.tensor_tensor(x1[:].rearrange("p t d -> p (t d)"), x1[:].rearrange("p t d -> p (t d)"), ps[:, 7, :], ALU.add).then_inc(f["y"].sem, 1)
            wait(e, f["y"], n, 1)
            xc = x_flat[:, bass.ds(c * CH, CH)]
            e.scalar_tensor_tensor(xc, x1[:].rearrange("p t d -> p (t d)"), 0.5, xc, ALU.mult, ALU.add).then_inc(f["x_done"].sem, 1)

        def dve_ret(e, n, c):
            def x_tile(t):
                return x_flat[:, bass.ds((c * CT + t) * D, D)]

            norm_stats(e, n, x_tile, st, mv, r["stat"])
            wait(e, r["stat"], n, 8)
            wait(e, r["rstd"], n, 1)
            for t in range(CT):
                e.tensor_scalar(z[:, t, :], x_tile(t), mv[:, t, 0:1], r1[:, t:t + 1], ALU.subtract, ALU.mult).then_inc(r["z"].sem, 1)
            for i in range(8):
                for k, (table, dst) in enumerate(((cos, ra), (sin, rb))):
                    m = 2 * i + k
                    wait(e, r["qkp"], n, m + 1)
                    if i >= 2:
                        wait(e, r["rot"], n, i - 1)
                    e.tensor_tensor(dst[:, i % 2, :].rearrange("p (b t) -> p b t", b=CB), ps[:, m % 8, :].rearrange("p (b t) -> p b t", b=CB),
                                    table[:].unsqueeze(1).broadcast_to([P, CB, SEQ]), ALU.mult).then_inc(r["rab"].sem, 1)
            for i in range(8):
                wait(e, r["th"], n, i + 1)
                e.scalar_tensor_tensor(sgT[:, i, :], th[:, i % 2, :], 1.0, ps[:, i, :], ALU.add, ALU.mult).then_inc(r["sgT"].sem, 1)

            def group_stats(u):
                b = u % 2
                wait(e, r["op"], n, u + 1)
                if u >= 2:
                    wait(e, r["ors"], n, u - 1)
                for q in range(2):
                    e.bn_stats(ost[:, b, q, :], ps[:, 2 + b, q * P:(q + 1) * P]).then_inc(r["ost"].sem, 1)
                for q in range(2):
                    wait_alone(e, r["ost"], n, 2 * u + q + 1)
                    e.bn_aggr(omv[:, b, q, :], ost[:, b, q, :]).then_inc(r["omv"].sem, 1)

            for u in range(16):
                wait(e, r["scp"], n, u + 1)
                if u >= 2:
                    wait(e, r["op"], n, u - 1)
                e.tensor_tensor(sc[:, u % 2, :], ps[:, u % 2, 0:3 * P], decay[:, u % HR, :], ALU.mult).then_inc(r["sc"].sem, 1)
                if u:
                    group_stats(u - 1)
            group_stats(15)
            wait(e, r["wop"], n, 1)
            xc = x_flat[:, bass.ds(c * CH, CH)]
            e.tensor_tensor(xc, ps[:, 6, :], xc, ALU.add).then_inc(r["x_done"].sem, 1)

        @block.vector
        def _(e):
            e.memset(wqp[:], 0.0).then_inc(spread.sem, 1)
            e.memset(wkp[:], 0.0).then_inc(spread.sem, 1)
            e.memset(bqp[:], 0.0).then_inc(spread.sem, 1)
            e.memset(one1[:], 1.0).then_inc(spread.sem, 1)
            e.wait_ge(spread.sem, 4)
            e.wait_ge(ld["w"], 16 * NLD_W)
            for k, wp in enumerate((wqp, wkp)):
                for part in range(3):
                    e.tensor_copy(wp[:, :, :, part, :], wqkv[:, k * D:(k + 1) * D].rearrange("p (g j k) -> p g j k", g=GA, k=DK)).then_inc(spread.sem, 1)
                    e.tensor_copy(bqp[:, k, :, :, part, :], bqkv[:, k * D:(k + 1) * D].rearrange("p (g j k) -> p g j k", g=GA, k=DK)).then_inc(spread.sem, 1)
            e.memset(bqp[:, 1, :, :, 3, 0:1], 1.0).then_inc(spread.sem, 1)
            e.wait_ge(ld["x"], 16)
            e.wait_ge(zeroed.sem, 4)
            e.wait_ge(vec_sb.sem, 2)
            with e.Fori(0, NCH) as c:
                dve_ffn(e, c, c)
            e.wait_ge(f["x_done"].sem, NCH)
            e.wait_ge(ld["r"], 16 * NLD_R)
            e.wait_ge(rw_sb.sem, 8)
            src = rw[:, 0:8, :].rearrange("p k (h a d) -> p (k h) a d", a=2, d=32)
            dst = rrot[:].rearrange("p k (h a d) -> p (k h) a d", a=2, d=32)
            e.tensor_scalar(dst[:, :, 0, :], src[:, :, 1, :], -1.0, None, ALU.mult).then_inc(rot_w.sem, 1)
            e.tensor_copy(dst[:, :, 1, :], src[:, :, 0, :]).then_inc(rot_w.sem, 1)
            with e.Fori(0, NCH) as c:
                dve_ret(e, c, c)
            e.wait_ge(r["x_done"].sem, NCH)
            with e.Fori(0, NCH) as c:
                dve_ffn(e, c + NCH, c)

        def act_ffn(e, n):
            wait(e, f["hTp"], n, 1)
            e.activation(hT[:], ps[:, 7, :], ACT.Identity, scale=vec[:, G1:G1 + 1], bias=vec[:, L1B:L1B + 1]).then_inc(f["hT"].sem, 1)
            for i in range(8):
                wait(e, f["qkp"], n, i + 1)
                if i >= 2:
                    wait(e, f["pack"], n, i - 1)
                e.activation(tqk[:, i % 2, :], ps[:, i % 4, :], ACT.Identity, bias=bqk[:, i % 2, i // 2:i // 2 + 1]).then_inc(f["tqk"].sem, 1)

            def evac_out(s):
                wait(e, f["pv"], n, 2 * s + 2)
                if s >= 2:
                    wait(e, f["oqp"], n, s - 1)
                e.activation(ou[:, s % 2, :], ps[:, 6, 0:SEQ], ACT.Identity).then_inc(f["ou"].sem, 1)

            for u in range(16):
                wait(e, f["st_ps"], n, u + 1)
                if u >= 2:
                    wait(e, f["pv"], n, u - 1)
                e.activation(pt[:, u % 2, :, :], ps[:, 4:6, :], ACT.Exp, scale=float(DK) ** -0.5).then_inc(f["pexp"].sem, 1)
                if u % 2 == 0 and u:
                    evac_out(u // 2 - 1)
            evac_out(7)
            wait(e, f["oTp"], n, 1)
            e.activation(oT[:], ps[:, 0, :], ACT.Identity).then_inc(f["oT"].sem, 1)
            wait(e, f["h2Tp"], n, 1)
            e.activation(h2T[:], ps[:, 2, :], ACT.Identity, scale=vec[:, G2:G2 + 1], bias=vec[:, L2B:L2B + 1]).then_inc(f["h2T"].sem, 1)
            for x in range(E):
                for k in range(FT):
                    wait(e, f["zps"], n, FT * x + k + 1)
                    if k == 0 and x >= 2:
                        wait(e, f["outp"], n, x - 1)
                    e.activation(hid[:, x % 2, k, :], ps[:, ZB[k], :], ACT.Relu, bias=vec[:, B1 + FT * x + k:B1 + FT * x + k + 1]).then_inc(f["hid"].sem, 1)
                    if x == 0 and k == 1:
                        wait(e, f["dv"], n, 1)
                        e.activation(ev[:], dv[:], ACT.Exp).then_inc(f["ev"].sem, 1)
                if x == 0:
                    wait(e, f["ewTp"], n, 1)
                    e.activation(ewT[:], ps[0:E, 6, :], ACT.Identity).then_inc(f["ewT"].sem, 1)
                wait(e, f["ewbp"], n, x + 1)
                if x >= 2:
                    wait(e, f["tmp"], n, x - 1)
                e.activation(ewb[:, x % 2, :], ps[:, 7, :], ACT.Identity).then_inc(f["ewb"].sem, 1)

        def act_ret(e, n):
            wait(e, r["zTp"], n, 1)
            e.activation(zT[:], ps[:, 7, :], ACT.Identity).then_inc(r["zT"].sem, 1)
            for i in range(8):
                wait(e, r["vp"], n, i + 1)
                e.activation(vr[:, i // 2, (i % 2) * 512:(i % 2 + 1) * 512], ps[:, i, :], ACT.Identity).then_inc(r["vr"].sem, 1)
            for i in range(8):
                wait(e, r["gp"], n, i + 1)
                if i >= 2:
                    wait(e, r["sgT"], n, i - 1)
                e.activation(th[:, i % 2, :], ps[:, i, :], ACT.Tanh, scale=0.5).then_inc(r["th"].sem, 1)

            def affine(u):
                h = u % HR
                wait(e, r["ohTp"], n, u + 1)
                if u >= 2:
                    wait(e, r["yT"], n, u - 1)
                e.activation(on[:, u % 2, :], ps[:, 4 + u % 2, 0:SEQ], ACT.Identity, scale=vec[:, GNW + h:GNW + h + 1],
                             bias=vec[:, GNB + h:GNB + h + 1]).then_inc(r["on"].sem, 1)

            for u in range(16):
                b = u % 2
                wait(e, r["ors"], n, u + 1)
                if u >= 2:
                    wait(e, r["ohTp"], n, u - 1)
                for q in range(2):
                    e.activation(oh[:, b, q, :], ps[:, 2 + b, q * P:(q + 1) * P], ACT.Identity, scale=ors[:, b, 1, q:q + 1],
                                 bias=ors[:, b, 3, q:q + 1]).then_inc(r["oh"].sem, 1)
                if u:
                    affine(u - 1)
            affine(15)

        @block.scalar
        def _(e):
            e.wait_ge(vec_ps.sem, 2)
            e.activation(vec[:], ps[:, 0, 0:52], ACT.Identity).then_inc(vec_sb.sem, 1)
            e.activation(bqk[:], ps[:, 1, 0:8].rearrange("p (k g) -> p k g", k=2), ACT.Identity).then_inc(vec_sb.sem, 1)
            e.wait_ge(vec_sb.sem, 2)
            with e.Fori(0, NCH) as c:
                act_ffn(e, c)
            for i in range(8):
                e.wait_ge(rw_ps.sem, i + 1)
                if i < 6:
                    e.activation(rw[:, 4 * i:4 * i + 4, :], ps[:, i, :].rearrange("p (k o) -> p k o", k=4), ACT.Identity).then_inc(rw_sb.sem, 1)
                else:
                    e.activation(rwo[:, 4 * (i - 6):4 * (i - 6) + 4, :], ps[:, i, :].rearrange("p (k o) -> p k o", k=4), ACT.Identity, scale=0.5).then_inc(rw_sb.sem, 1)
            with e.Fori(0, NCH) as c:
                act_ret(e, c)
            with e.Fori(0, NCH) as c:
                act_ffn(e, c + NCH)

        def transposes(e, dst, src, sig):
            for t in range(CT):
                last = e.transpose(dst(t), src(t), ident[:])
            last.then_inc(sig.sem, 1)

        def pe_ffn(e, n):
            wait(e, f["z"], n, 4)
            transposes(e, lambda t: ps[:, 7, t * P:(t + 1) * P], lambda t: z[:, t, :], f["hTp"])
            wait(e, f["hT"], n, 1)
            for i in range(8):
                if i >= 4:
                    wait(e, f["tqk"], n, i - 3)
                wp = (wkp if i % 2 else wqp)[:, i // 2, :, :, :].rearrange("p j a k -> p (j a k)")
                e.matmul(ps[:, i % 4, :], wp, hT[:], start=True, stop=True).then_inc(f["qkp"].sem, 1)
            for t in range(CT):
                last = e.matmul(ps[:, 4, t * D:(t + 1) * D], hT[:, t * P:(t + 1) * P], wqkv[:, 2 * D:], start=True, stop=True)
            last.then_inc(f["vps"].sem, 1)

            def scores(s, pr):
                bb, g = divmod(s, GA)
                lo = bb * SEQ
                if s == 0:
                    wait(e, f["pack"], n, 8)
                else:
                    wait(e, f["smax"], n, 2 * s + pr - 1)
                for q in range(2):
                    for jj in range(2):
                        j = 32 * (2 * pr + jj)
                        last = e.matmul(ps[:, 2 * pr + jj, q * SEQ:(q + 1) * SEQ], qp[j:j + 32, g, lo + q * P:lo + (q + 1) * P],
                                        kp[j:j + 32, g, lo:lo + SEQ], start=True, stop=True)
                last.then_inc(f["s_ps"].sem, 1)

            def scores_t(s, pr):
                bb, g = divmod(s, GA)
                lo = bb * SEQ
                u = 2 * s + pr
                if u == 0:
                    wait(e, f["vaug"], n, 1)
                else:
                    wait(e, f["pexp"], n, u)
                if pr == 0:
                    wait(e, f["qm"], n, s + 1)
                for q in range(2):
                    for jj in range(2):
                        j = 32 * (2 * pr + jj)
                        last = e.matmul(ps[:, 4 + jj, q * SEQ:(q + 1) * SEQ], kp[j:j + 32, g, lo + q * P:lo + (q + 1) * P],
                                        qm[j:j + 32, s % 2, :], start=True, stop=True)
                last.then_inc(f["st_ps"].sem, 1)

            def values(s, pr):
                bb, g = divmod(s, GA)
                u = 2 * s + pr
                wait(e, f["pexp"], n, u + 1)
                if pr == 0 and s:
                    wait(e, f["ou"], n, s)
                for jj in range(2):
                    j = 2 * pr + jj
                    for k in range(2):
                        last = e.matmul(ps[32 * j:32 * j + 32, 6, 0:SEQ], vaug[:, 2 * bb + k, 4 * g + j, :], pt[:, u % 2, jj, k * SEQ:(k + 1) * SEQ],
                                        start=(k == 0), stop=(k == 1), tile_position=(0, 32 * j))
                last.then_inc(f["pv"].sem, 1)

            def out_t(s):
                wait(e, f["ou"], n, s + 1)
                wait(e, f["qm"], n, min(s + 2, 8))
                for q in range(2):
                    last = e.transpose(ps[:, 7, q * P:(q + 1) * P], ou[:, s % 2, q * P:(q + 1) * P], ident[:])
                last.then_inc(f["oqp"].sem, 1)

            scores(0, 0)
            scores(0, 1)
            for s in range(8):
                wait(e, f["smax"], n, 2 * s + 2)
                if s >= 2:
                    wait(e, f["o_tm"], n, s - 1)
                for q in range(2):
                    last = e.transpose(ps[:, 7, q * P:(q + 1) * P], msp[:, s % 2, q, :], ident[:])
                last.then_inc(f["mTp"].sem, 1)
                if s < 7:
                    scores(s + 1, 0)
                    scores(s + 1, 1)
                scores_t(s, 0)
                if s:
                    values(s - 1, 1)
                scores_t(s, 1)
                values(s, 0)
                if s:
                    out_t(s - 1)
            values(7, 1)
            wait(e, f["o_tm"], n, 7)
            out_t(7)
            wait(e, f["o_tm"], n, 8)
            transposes(e, lambda t: ps[:, 0, t * P:(t + 1) * P], lambda t: o_tm[:, t, :], f["oTp"])
            wait(e, f["oT"], n, 1)
            for t in range(CT):
                last = e.matmul(ps[:, 1, t * D:(t + 1) * D], oT[:, t * P:(t + 1) * P], wo[:], start=True, stop=True)
            last.then_inc(f["x1p"].sem, 1)
            wait(e, f["z2"], n, 4)
            transposes(e, lambda t: ps[:, 2, t * P:(t + 1) * P], lambda t: z2[:, t, :], f["h2Tp"])
            wait(e, f["h2T"], n, 1)
            for t in range(CT):
                last = e.matmul(ps[:, 3, t * E:(t + 1) * E], h2T[:, t * P:(t + 1) * P], gate_w[:], start=True, stop=True)
            last.then_inc(f["lgp"].sem, 1)

            def up(x):
                for k in range(FT):
                    if x:
                        wait(e, f["hid"], n, FT * (x - 1) + k + 1)
                    e.matmul(ps[:, ZB[k], :], w1[:, x, k * P:(k + 1) * P], h2T[:], start=True, stop=True).then_inc(f["zps"].sem, 1)

            def spread_weight(x):
                if x:
                    wait(e, f["ewb"], n, x)
                e.matmul(ps[:, 7, :], sel[:, x, :], ewT[:], start=True, stop=True).then_inc(f["ewbp"].sem, 1)

            e.wait_ge(ld["moe"], 16 * NLD_MOE)
            up(0)
            wait(e, f["ew"], n, 1)
            for t in range(CT):
                last = e.transpose(ps[0:E, 6, t * P:(t + 1) * P], ew[:, t, :], ident[:])
            last.then_inc(f["ewTp"].sem, 1)
            wait(e, f["ewT"], n, 1)
            spread_weight(0)
            e.matmul(ps[:, 6, :], b2[:], ewT[:], start=True, stop=True).then_inc(f["b2p"].sem, 1)
            for x in range(E):
                if x + 1 < E:
                    up(x + 1)
                    spread_weight(x + 1)
                wait(e, f["hid"], n, FT * (x + 1))
                if x >= 2:
                    wait(e, f["tmp"], n, x - 1)
                for k in range(FT):
                    last = e.matmul(ps[:, 2 + x % 2, :], w2[:, x, k, :], hid[:, x % 2, k, :], start=(k == 0), stop=(k == FT - 1))
                last.then_inc(f["outp"].sem, 1)
            wait(e, f["acc"], n, 8)
            wait(e, f["ewb"], n, 8)
            transposes(e, lambda t: ps[:, 7, t * P:(t + 1) * P], lambda t: acc[:, t * P:(t + 1) * P], f["accTp"])

        def pe_ret(e, n):
            wait(e, r["z"], n, 4)
            transposes(e, lambda t: ps[:, 7, t * P:(t + 1) * P], lambda t: z[:, t, :], r["zTp"])
            wait(e, r["zT"], n, 1)
            for m in range(16):
                hp, k = divmod(m, 4)
                if m >= 8:
                    wait(e, r["rab"], n, m - 7)
                w = (rrot if k % 2 else rw)[:, hp + 4 * (k // 2), :]
                e.matmul(ps[:, m % 8, :], w, zT[:], start=True, stop=True).then_inc(r["qkp"].sem, 1)
            for i in range(8):
                wait(e, r["rab"], n, 9 + i)
                t, half = divmod(i, 2)
                w = rw[:, 8 + 4 * half:12 + 4 * half, :].rearrange("p k o -> p (k o)")
                e.matmul(ps[:, i, :], zT[:, t * P:(t + 1) * P], w, start=True, stop=True).then_inc(r["vp"].sem, 1)
            for i in range(8):
                wait(e, r["vr"], n, i + 1)
                e.matmul(ps[:, i, :], rw[:, 16 + i, :], zT[:], start=True, stop=True).then_inc(r["gp"].sem, 1)

            def scores(u):
                bb, h = divmod(u, HR)
                j, hp, lo = 64 * (h % 2), h // 2, bb * SEQ
                if u == 0:
                    wait(e, r["rot"], n, 8)
                if u < 2:
                    wait(e, r["sgT"], n, 8)
                else:
                    wait(e, r["sc"], n, u - 1)
                e.matmul(ps[:, u % 2, 0:SEQ], kr[j:j + DR, hp, lo:lo + P], qr[j:j + DR, hp, lo:lo + SEQ], start=True, stop=True)
                e.matmul(ps[:, u % 2, SEQ:SEQ + P], kr[j:j + DR, hp, lo + P:lo + SEQ], qr[j:j + DR, hp, lo + P:lo + SEQ],
                         start=True, stop=True).then_inc(r["scp"].sem, 1)

            def values(u):
                bb, h = divmod(u, HR)
                b = u % 2
                wait(e, r["sc"], n, u + 1)
                if u >= 2:
                    wait(e, r["oh"], n, 2 * u - 2)
                v = [vr[:, 2 * bb + k, h * P:(h + 1) * P] for k in range(2)]
                e.matmul(ps[:, 2 + b, 0:P], sc[:, b, 0:P], v[0], start=True, stop=True)
                e.matmul(ps[:, 2 + b, P:2 * P], sc[:, b, P:2 * P], v[0], start=True, stop=False)
                e.matmul(ps[:, 2 + b, P:2 * P], sc[:, b, 2 * P:3 * P], v[1], start=False, stop=True).then_inc(r["op"].sem, 1)

            def normed_t(u):
                b = u % 2
                wait(e, r["oh"], n, 2 * u + 2)
                if u >= 2:
                    wait(e, r["on"], n, u - 1)
                for q in range(2):
                    last = e.transpose(ps[:, 4 + b, q * P:(q + 1) * P], oh[:, b, q, :], ident[:])
                last.then_inc(r["ohTp"].sem, 1)

            for u in range(18):
                if u < 16:
                    scores(u)
                if 1 <= u <= 16:
                    values(u - 1)
                if u >= 2:
                    normed_t(u - 2)
            wait(e, r["yT"], n, 16)
            for t in range(CT):
                for h in range(HR):
                    last = e.matmul(ps[:, 6, t * D:(t + 1) * D], yT[:, h, t * P:(t + 1) * P], rwo[:, h, :], start=(h == 0), stop=(h == HR - 1))
            last.then_inc(r["wop"].sem, 1)

        @block.tensor
        def _(e):
            e.wait_ge(ld["w"], 16 * NLD_W)
            e.transpose(ps[:, 0, 0:52], vec_rows[:], ident[0:52, 0:52]).then_inc(vec_ps.sem, 1)
            e.wait_ge(spread.sem, 17)
            for k in range(2):
                for g in range(GA):
                    last = e.matmul(ps[:, 1, 4 * k + g:4 * k + g + 1], bqp[:, k, g, :, :, :].rearrange("p j a k -> p (j a k)"), one1[:], start=True, stop=True)
            last.then_inc(vec_ps.sem, 1)
            e.wait_ge(vec_sb.sem, 2)
            e.wait_ge(zeroed.sem, 4)
            with e.Fori(0, NCH) as c:
                pe_ffn(e, c)
            e.wait_ge(ld["r"], 16 * NLD_R)
            e.wait_ge(f["x_done"].sem, NCH)
            for i in range(8):
                for k in range(4):
                    src = ret_in[:, 4 * i + k, :] if i < 6 else wo_in[:, (4 * (i - 6) + k) * P:(4 * (i - 6) + k + 1) * P]
                    last = e.transpose(ps[:, i, k * P:(k + 1) * P], src, ident[:])
                last.then_inc(rw_ps.sem, 1)
            e.wait_ge(rw_sb.sem, 8)
            e.wait_ge(rot_w.sem, 2)
            with e.Fori(0, NCH) as c:
                pe_ret(e, c)
            with e.Fori(0, NCH) as c:
                pe_ffn(e, c + NCH)


ZB = (0, 1, 4, 5)


def kernel(**inputs):
    import concourse.bacc as bacc
    from concourse.bass_utils import run_bass_kernel_spmd as run

    x = np.asarray(inputs["L0_attn_x"])
    nc = bacc.Bacc("TRN2", target_bir_lowering=False, num_devices=1)
    arrays, aps = {}, {}
    for name, v in {**inputs, **constants(x.shape[0] * x.shape[1] // P)}.items():
        v = np.ascontiguousarray(v)
        arrays["in_" + name] = v
        aps[name] = nc.dram_tensor("in_" + name, v.shape, mybir.dt.from_np(v.dtype), kind="ExternalInput").ap()
    out = nc.dram_tensor("out_x", x.shape, F32, kind="ExternalOutput").ap()
    build(nc, aps, out)
    return run(nc, [arrays], core_ids=[0]).results[0]["out_x"]
```

```python
from contextlib import ExitStack

import numpy as np
import concourse.bass as bass
from concourse import mybir

F32 = mybir.dt.float32
F32R = mybir.dt.float32r
U32 = mybir.dt.uint32
ALU = mybir.AluOpType
ACT = mybir.ActivationFunctionType
AX = mybir.AxisListType

P = 128
SEQ = 256
D = 128
CT = 4
CH = CT * P
CB = CH // SEQ
EPS = 1e-5
HA, DK = 16, 8
GA = 4
E, FT = 8, 4
HR, DR = 8, 64
AUG = 24


class Signal:

    def __init__(self, sem, per):
        self.sem, self.per = sem, per

    def __call__(self, n, k):
        return n * self.per + k


def constants(NT):
    inv = (1.0 / np.float32(10000.0) ** (np.arange(0, DR, 2, dtype=np.float32) / np.float32(DR))).astype(np.float32)
    fr = np.arange(SEQ, dtype=np.float32)[:, None] * inv[None, :]
    emb = np.concatenate([fr, fr], -1)
    cos = np.tile(np.cos(emb).T, (2, 1)).astype(np.float32)
    sin = np.tile(np.sin(emb).T, (2, 1)).astype(np.float32)
    gamma = 1.0 - np.exp2(-5.0 - np.arange(HR, dtype=np.float64))
    s = np.arange(P)[:, None]
    dec = np.zeros((P, HR, 3 * P))
    for h in range(HR):
        rel = np.arange(P)[None, :] - s
        diag = np.where(rel >= 0, gamma[h] ** np.maximum(rel, 0), 0.0)
        dec[:, h, 0:P] = diag
        dec[:, h, P:2 * P] = gamma[h] ** (rel + P)
        dec[:, h, 2 * P:] = diag
    dec *= DR ** -0.5
    mask = np.zeros((P, 2), np.float32)
    for j in range(4):
        mask[32 * j + 16:32 * j + 24, 0] = -1.0
        mask[32 * j + 8:32 * j + 16, 1] = -1.0
    return {
        "c_ident": np.eye(P, dtype=np.float32), "c_cos": cos, "c_sin": sin,
        "c_decay": dec.astype(np.float32).reshape(P, HR * 3 * P),
        "c_iota": np.tile(np.arange(E, dtype=np.float32), (P, 1)), "c_mask": mask,
    }


def build(nc, a, out):
    x_d = a["L0_attn_x"]
    NTOK = x_d.shape[0] * x_d.shape[1]
    NT = NTOK // P
    NCH = NTOK // CH
    ctx = ExitStack()
    scope = [ctx]
    with ctx:
        def sb(name, shape, dt=F32):
            return scope[0].enter_context(nc.sbuf_tensor(name, shape, dt))

        def sg(name, per):
            return Signal(ctx.enter_context(nc.semaphore(name)), per)

        x_sb = sb("x_sb", [P, NT, D])
        w1 = sb("w1", [P, E, FT * P])
        w2 = sb("w2", [P, E, FT, D])
        wqkv = sb("wqkv", [P, 3 * D])
        wqp = sb("wqp", [P, GA, 4, 4, DK])
        wkp = sb("wkp", [P, GA, 4, 4, DK])
        wo = sb("wo", [P, D])
        gate_w = sb("gate_w", [P, E])
        b2 = sb("b2", [E, D])
        bqkv = sb("bqkv", [1, 3 * D])
        bqp = sb("bqp", [1, 2, GA, 4, 4, DK])
        one1 = sb("one1", [1, 1])
        bqk = sb("bqk", [P, 2, GA])
        bv_bc = sb("bv_bc", [P, D])
        bo_bc = sb("bo_bc", [P, D])
        gb_bc = sb("gb_bc", [P, E])
        vec_rows = sb("vec_rows", [52, P])
        vec = sb("vec", [P, 52])
        ident = sb("ident", [P, P])
        cos = sb("cos", [P, SEQ])
        sin = sb("sin", [P, SEQ])
        decay = sb("decay", [P, HR, 3 * P])
        iota = sb("iota", [P, E])
        mask = sb("mask", [P, 2])
        ret_in = sb("ret_in", [P, 24, P])
        wo_in = sb("wo_in", [P, HR * P])
        rw = sb("rw", [P, 24, P])
        rrot = sb("rrot", [P, 8, P])
        rwo = sb("rwo", [P, HR, D])
        mhalf = sb("mhalf", [P, CT])
        B1, GNW, GNB, G1, L1B, G2, L2B = 0, 32, 40, 48, 49, 50, 51

        vaug = sb("vaug", [P, CT, HA, 32])
        msp = sb("msp", [P, 2, 2, P])
        ln_t = sb("ln_t", [P, 6, CT])
        st = sb("st", [P, CT, 6])
        mv = sb("mv", [P, CT, 2])
        r1 = sb("r1", [P, CT])
        r12 = sb("r12", [P, CT])
        z = sb("z", [P, CT, D])
        ffn_only = ExitStack()
        scope[0] = ffn_only
        xn = sb("xn", [P, CT, D])
        hT = sb("hT", [P, CH])
        tqk = sb("tqk", [P, 2, CH])
        hi = sb("hi", [P, 2, CH], F32R)
        qp = sb("qp", [P, GA, CH], F32R)
        kp = sb("kp", [P, GA, CH], F32R)
        qm = sb("qm", [P, 2, SEQ], F32R)
        pt = sb("pt", [P, 2, 2, 2 * SEQ])
        ou = sb("ou", [P, 2, SEQ])
        rec = sb("rec", [P, 2, 2, 4])
        o_tm = sb("o_tm", [P, CT, D])
        oT = sb("oT", [P, CH])
        x1 = sb("x1", [P, CT, D])
        st2 = sb("st2", [P, CT, 6])
        mv2 = sb("mv2", [P, CT, 2])
        r2 = sb("r2", [P, CT])
        h2n = sb("h2n", [P, CH])
        h2T = sb("h2T", [P, CH])
        lg = sb("lg", [P, CT, E])
        top = sb("top", [P, CT, 8])
        tix = sb("tix", [P, CT, 8], U32)
        tif = sb("tif", [P, CT, 2])
        dv = sb("dv", [P, CT])
        ev = sb("ev", [P, CT])
        den = sb("den", [P, CT])
        gw1 = sb("gw1", [P, CT])
        gw2 = sb("gw2", [P, CT])
        ew_a = sb("ew_a", [P, CT, E])
        ew_b = sb("ew_b", [P, CT, E])
        ewn = sb("ewn", [P, CT, E])
        ew = sb("ew", [P, CT, E])
        ewT = sb("ewT", [E, CH])
        hid = sb("hid", [P, 2, FT, CH])
        tmp = sb("tmp", [P, 2, CH])
        ffn_only.close()
        scope[0] = ctx
        zT = sb("zT", [P, CH])
        ra = sb("ra", [P, 2, CH])
        rb = sb("rb", [P, 2, CH])
        qr = sb("qr", [P, 4, CH])
        kr = sb("kr", [P, 4, CH])
        vr = sb("vr", [P, CT, HR * P])
        th = sb("th", [P, 2, CH])
        sgT = sb("sgT", [P, HR, CH])
        sc = sb("sc", [P, 2, 3 * P])
        ost = sb("ost", [P, 2, 2, 6])
        omv = sb("omv", [P, 2, 2, 2])
        ors = sb("ors", [P, 2, 4, 2])
        oh = sb("oh", [P, 2, 2, P])
        on = sb("on", [P, 2, SEQ])
        yT = sb("yT", [P, HR, CH])

        ps = ctx.enter_context(nc.psum_tensor("ps", [P, 8, 512], F32))

        ld = {k: ctx.enter_context(nc.semaphore("ld_" + k)) for k in ("x", "w", "r", "moe")}
        zeroed = sg("zeroed", 0)
        spread = sg("spread", 0)
        vec_ps = sg("vec_ps", 0)
        vec_sb = sg("vec_sb", 0)
        rw_ps = sg("rw_ps", 0)
        rw_sb = sg("rw_sb", 0)
        rot_w = sg("rot_w", 0)
        f = {k: sg("f_" + k, v) for k, v in dict(
            stat=8, rstd=1, xn=4, z=4, xnb=1, hTp=1, hT=1, qkp=8, tqk=8, hi=8, pack=8, vps=1, vaug=1,
            s_ps=16, smax=16, mTp=8, qm=8, st_ps=16, pexp=16, pv=16, ou=8, oqp=8, rec=8, o_tm=8, oTp=1, oT=1,
            x1p=1, x1=1, stat2=8, rstd2=1, z2=4, h2Tp=1, h2n=1, h2T=1, lgp=1, lg=1, top=4, tix=4, dv=2, ev=1, gw=3, ewab=8,
            ewn=1, ew=1, ewTp=1, ewT=1, half=1, b2p=1, acc0=1, zps=32, hid=32, outp=8, tmp=8, acc=7, x_done=1, chain=6, chain2=1).items()}
        r = {k: sg("r_" + k, v) for k, v in dict(
            stat=8, rstd=1, z=4, zTp=1, zT=1, qkp=16, rab=16, rot=8, vp=8, vr=8, gp=8, th=8, sgT=8,
            scp=16, sc=16, op=16, ost=32, omv=32, ors=16, oh=32, ohTp=16, on=16, yT=16, wop=1, x_done=1,
            chain=1 + 16 * 3).items()}
        stored = ctx.enter_context(nc.semaphore("stored"))
        passed = ctx.enter_context(nc.semaphore("passed"))
        x_flat = x_sb[:].rearrange("p n d -> p (n d)")
        x_tok = x_d.rearrange("b (t p) d -> p (b t) d", p=P)
        out_tok = out.rearrange("b (t p) d -> p (b t) d", p=P)
        NLD_W, NLD_MOE, NLD_R = 17, 3, 8

        block = ctx.enter_context(nc.Block())

        def run_ffn(e, eng, rnd):
            n0 = rnd * NCH
            eng.pre(e, n0, 0)
            eng.turn(e, n0 - 1, -1, False, True, False)
            eng.steps(e, n0, 0, False, True)
            eng.turn(e, n0, 0, True, True, False)
            with e.Fori(1, NCH - 1) as c:
                eng.steps(e, c + n0, c, True, True)
                eng.turn(e, c + n0, c, True, True, True)
            last = n0 + NCH - 1
            eng.steps(e, last, NCH - 1, True, False)
            eng.turn(e, last, NCH - 1, True, False, True)
            eng.experts(e, last, NCH - 1)

        PIECES = 4 * (E + 1)
        START, FILL = 2, 3
        REST = START + 8 * FILL

        def filler(first, on, do):
            piece = first

            def fill(many):
                nonlocal piece
                for _ in range(many if on else 0):
                    do(piece)
                    piece += 1
            return fill

        def finishes(piece):
            return piece >= 4 and piece % 4 == 3

        def wait(e, sig, n, k):
            e.wait_ge(sig.sem, sig(n, k))

        def wait_alone(e, sig, n, k):
            e.wait_ge(sig.sem, sig(n, k))
            e.sem_inc(passed)

        @block.sync
        def _(e):
            e.dma_start(x_sb[:], x_tok).then_inc(ld["x"], 16)
            for dst, src in (
                (ident[:], a["c_ident"]), (wqkv[:], a["L0_ffn_w_qkv"]),
                (bqkv[:], a["L0_ffn_b_qkv"].unsqueeze(0)),
                (vec_rows[B1:B1 + 32, :], a["L0_ffn_b1"].rearrange("e (k f) -> (e k) f", f=P)),
                (vec_rows[GNW:GNW + 8, :], a["L0_attn_gn_weight"].rearrange("(h f) -> h f", f=P)),
                (vec_rows[GNB:GNB + 8, :], a["L0_attn_gn_bias"].rearrange("(h f) -> h f", f=P)),
                (vec_rows[G1:G1 + 1, :], a["L0_ffn_ln1_g"].unsqueeze(0)),
                (vec_rows[L1B:L1B + 1, :], a["L0_ffn_ln1_b"].unsqueeze(0)),
                (vec_rows[G2:G2 + 1, :], a["L0_ffn_ln2_g"].unsqueeze(0)),
                (vec_rows[L2B:L2B + 1, :], a["L0_ffn_ln2_b"].unsqueeze(0)),
                (mask[:], a["c_mask"]), (iota[:], a["c_iota"]),
                (bv_bc[:], a["L0_ffn_b_qkv"][2 * D:3 * D].partition_broadcast(P)),
                (bo_bc[:], a["L0_ffn_b_o"].partition_broadcast(P)),
                (gb_bc[:], a["L0_ffn_gate_b"].partition_broadcast(P)),
                (wo[:], a["L0_ffn_w_o"]), (gate_w[:], a["L0_ffn_gate_w"]),
            ):
                e.dma_start(dst, src).then_inc(ld["w"], 16)
            e.dma_start(w1[:], a["L0_ffn_W1"].rearrange("e d f -> d e f")).then_inc(ld["moe"], 16)
            e.dma_start(w2[:], a["L0_ffn_W2"].rearrange("e (k f) d -> f e k d", f=P)).then_inc(ld["moe"], 16)
            e.dma_start(b2[:], a["L0_ffn_b2"]).then_inc(ld["moe"], 16)
            for name, at in (("Wq", 0), ("Wk", 4), ("Wv", 8), ("Wg", 16)):
                w = a["L0_attn_" + name].rearrange("(k o) i -> o k i", o=P)
                e.dma_start(ret_in[:, at:at + w.shape[1], :], w).then_inc(ld["r"], 16)
            e.dma_start(wo_in[:], a["L0_attn_Wo"]).then_inc(ld["r"], 16)
            e.dma_start(decay[:], a["c_decay"].rearrange("p (h k) -> p h k", h=HR)).then_inc(ld["r"], 16)
            e.dma_start(cos[:], a["c_cos"]).then_inc(ld["r"], 16)
            e.dma_start(sin[:], a["c_sin"]).then_inc(ld["r"], 16)
            with e.Fori(0, NCH) as c:
                wait(e, f["x_done"], c + NCH, 1)
                e.dma_start(out_tok[:, bass.ds(c * CT, CT), :], x_sb[:, bass.ds(c * CT, CT), :]).then_inc(stored, 16)
            e.wait_ge(stored, 16 * NCH)

        def rsqrt_chain(e, steps, chain, n, k0, last):
            for i, ins in enumerate(steps):
                if i:
                    wait_alone(e, chain, n, k0 + i)
                done = ins()
                if i + 1 < len(steps):
                    done.then_inc(chain.sem, 1)
            done.then_inc(last.sem, 1)

        def pool_tt(e, o, a0, a1, op):
            return lambda: e.tensor_tensor(o, a0, a1, op)

        def pool_ve(e, o, v):
            return lambda: e.tensor_scalar(o, v, 1.0, EPS, ALU.mult, ALU.add)

        class PoolFfn:
            @staticmethod
            def pre(e, n, c):
                wait_alone(e, f["stat"], n, 8)
                rsqrt_chain(e, [
                    pool_ve(e, ln_t[:, 0, :], mv[:, :, 1]),
                    pool_tt(e, r1[:], ln_t[:, 0, :], mhalf[:], ALU.pow),
                    pool_tt(e, ln_t[:, 1, :], r1[:], r1[:], ALU.mult),
                    pool_tt(e, ln_t[:, 2, :], ln_t[:, 1, :], mv[:, :, 1], ALU.mult),
                    pool_ve(e, ln_t[:, 3, :], ln_t[:, 2, :]),
                    pool_tt(e, ln_t[:, 4, :], ln_t[:, 3, :], mhalf[:], ALU.pow),
                    pool_tt(e, r12[:], r1[:], ln_t[:, 4, :], ALU.mult)], f["chain"], n, 0, f["rstd"])

            @staticmethod
            def turn(e, n, c, tail, head, moe):
                fill = filler(REST, moe, lambda piece: PoolFfn.piece(e, n - 1, c - 1, piece))
                fill(3)
                if tail:
                    wait_alone(e, f["stat2"], n, 8)
                    rsqrt_chain(e, [
                        pool_ve(e, ln_t[:, 5, :], mv2[:, :, 1]),
                        pool_tt(e, r2[:], ln_t[:, 5, :], mhalf[:], ALU.pow)], f["chain2"], n, 0, f["rstd2"])
                fill(3)
                if head:
                    wait(e, f["xn"], n + 1, 4)
                    e.tensor_tensor(xn[:], xn[:], bo_bc[:].unsqueeze(1).broadcast_to([P, CT, D]), ALU.add).then_inc(f["xnb"].sem, 1)
                fill(PIECES - REST - 6)

            @staticmethod
            def piece(e, n, c, piece):
                if not finishes(piece):
                    return
                x = piece // 4 - 1
                wait(e, f["tmp"], n, x + 1)
                wait_alone(e, f["acc"] if x else f["acc0"], n, x or 1)
                xc = x_flat[:, bass.ds(c * CH, CH)]
                e.tensor_tensor(xc, xc, tmp[:, x % 2, :], ALU.add).then_inc((f["acc"] if x < E - 1 else f["x_done"]).sem, 1)

            @staticmethod
            def steps(e, n, c, moe, ahead):
                fill = filler(0, moe, lambda piece: PoolFfn.piece(e, n - 1, c - 1, piece))
                fill(START + 6 * FILL)
                if ahead:
                    PoolFfn.pre(e, n + 1, c + 1)
                fill(2 * FILL)

            @staticmethod
            def experts(e, n, c):
                for piece in range(PIECES):
                    PoolFfn.piece(e, n, c, piece)

        def pool_ret(e, n):
            wait_alone(e, r["stat"], n, 8)
            rsqrt_chain(e, [
                pool_ve(e, ln_t[:, 0, :], mv[:, :, 1]),
                pool_tt(e, r1[:], ln_t[:, 0, :], mhalf[:], ALU.pow)], r["chain"], n, 0, r["rstd"])
            for i in range(8):
                wait(e, r["rab"], n, 2 * i + 2)
                e.tensor_tensor((kr if i % 2 else qr)[:, i // 2, :], ra[:, i % 2, :], rb[:, i % 2, :], ALU.add).then_inc(r["rot"].sem, 1)

            def gated(u):
                wait(e, r["on"], n, u + 1)
                h, lo = u % HR, u // HR * SEQ
                e.tensor_tensor(yT[:, h, lo:lo + SEQ], on[:, u % 2, :], sgT[:, h, lo:lo + SEQ], ALU.mult).then_inc(r["yT"].sem, 1)

            wait(e, r["sgT"], n, 8)
            for u in range(16):
                b = u % 2
                if u >= 2:
                    wait(e, r["oh"], n, 2 * u - 2)
                wait_alone(e, r["omv"], n, 2 * u + 2)
                rsqrt_chain(e, [
                    pool_ve(e, ors[:, b, 0, :], omv[:, b, :, 1]),
                    pool_tt(e, ors[:, b, 1, :], ors[:, b, 0, :], mhalf[:, 0:2], ALU.pow),
                    lambda: e.tensor_tensor(ors[:, b, 2, :], ors[:, b, 1, :], omv[:, b, :, 0], ALU.mult),
                    lambda: e.tensor_scalar(ors[:, b, 3, :], ors[:, b, 2, :], -1.0, 1.0, ALU.mult, ALU.mult)], r["chain"], n, 1 + 3 * u, r["ors"])
                if u:
                    gated(u - 1)
            gated(15)

        @block.gpsimd
        def _(e):
            e.memset(mhalf[:], -0.5).then_inc(zeroed.sem, 1)
            e.memset(vaug[:], 0.0).then_inc(zeroed.sem, 1)
            e.memset(msp[:], 0.0).then_inc(zeroed.sem, 1)
            e.wait_ge(zeroed.sem, 3)
            e.memset(vaug[:, :, :, DK:DK + 1], 1.0).then_inc(zeroed.sem, 1)
            e.wait_ge(ld["w"], 16 * NLD_W)
            run_ffn(e, PoolFfn, 0)
            with e.Fori(0, NCH) as c:
                pool_ret(e, c)
            run_ffn(e, PoolFfn, 1)

        def norm_stats(e, n, src, s_, m_, sig):
            for t in range(CT):
                e.bn_stats(s_[:, t, :], src(t)).then_inc(sig.sem, 1)
            for t in range(CT):
                wait_alone(e, sig, n, t + 1)
                e.bn_aggr(m_[:, t, :], s_[:, t, :]).then_inc(sig.sem, 1)

        class DveFfn:
            @staticmethod
            def stats(e, n, c):
                norm_stats(e, n, lambda t: x_flat[:, bass.ds((c * CT + t) * D, D)], st, mv, f["stat"])

            @staticmethod
            def rows(e, n, c):
                wait(e, f["stat"], n, 8)
                wait(e, f["rstd"], n, 1)
                for t in range(CT):
                    e.tensor_scalar(z[:, t, :], x_flat[:, bass.ds((c * CT + t) * D, D)], mv[:, t, 0:1], r12[:, t:t + 1],
                                    ALU.subtract, ALU.mult).then_inc(f["z"].sem, 1)

            @staticmethod
            def pre(e, n, c):
                DveFfn.stats(e, n, c)
                DveFfn.rows(e, n, c)

            @staticmethod
            def weigh(e, n, s):
                bb, g = divmod(s, GA)
                wait(e, f["oqp"], n, s + 1)
                o = ps[:, 5, 0:SEQ].rearrange("p (q j k) -> p q j k", q=2, k=32)
                e.reciprocal(rec[:, s % 2, :, :], o[:, :, :, DK]).then_inc(f["rec"].sem, 1)
                wait(e, f["rec"], n, s + 1)
                e.tensor_tensor(o_tm[:, 2 * bb:2 * bb + 2, 32 * g:32 * g + 32].rearrange("p q (j k) -> p q j k", k=DK), o[:, :, :, 0:DK],
                                rec[:, s % 2, :, :].unsqueeze(3).broadcast_to([P, 2, 4, DK]), ALU.mult).then_inc(f["o_tm"].sem, 1)

            @staticmethod
            def biggest(e, n, s):
                for pr in range(2):
                    wait(e, f["s_ps"], n, 2 * s + pr + 1)
                    e.tensor_reduce(msp[:, s % 2, :, 64 * pr + AUG:64 * pr + AUG + 33:32].rearrange("p q j -> p j q"),
                                    ps[:, 0:2, :].rearrange("p j (q k) -> p j q k", q=2), AX.X, ALU.max, negate=True).then_inc(f["smax"].sem, 1)

            @staticmethod
            def piece(e, n, piece):
                if not finishes(piece):
                    return
                x = piece // 4 - 1
                wait(e, f["outp"], n, x + 1)
                if x == 0:
                    wait(e, f["ew"], n, 1)
                if x:
                    wait(e, f["acc"], n, max(x - 1, 1))
                e.tensor_tensor(tmp[:, x % 2, :].rearrange("p (t d) -> p t d", d=D), ps[:, 7, :].rearrange("p (t d) -> p t d", d=D),
                                ew[:, :, x:x + 1].broadcast_to([P, CT, D]), ALU.mult).then_inc(f["tmp"].sem, 1)

            @staticmethod
            def steps(e, n, c, moe, ahead):
                fill = filler(0, moe, lambda piece: DveFfn.piece(e, n - 1, piece))
                DveFfn.biggest(e, n, 0)
                fill(START)
                for s in range(8):
                    bb, g = divmod(s, GA)
                    wait(e, f["mTp"], n, s + 1)
                    e.tensor_tensor(qm[:, s % 2, :], ps[:, 5, 0:SEQ], qp[:, g, bb * SEQ:(bb + 1) * SEQ].bitcast(F32), ALU.add).then_inc(f["qm"].sem, 1)
                    if ahead and s == 5:
                        DveFfn.stats(e, n + 1, c + 1)
                    if ahead and s == 6:
                        DveFfn.rows(e, n + 1, c + 1)
                    if s < 7:
                        DveFfn.biggest(e, n, s + 1)
                    fill(FILL - 1)
                    if s:
                        DveFfn.weigh(e, n, s - 1)
                    fill(1)

            @staticmethod
            def turn(e, n, c, tail, head, moe):
                fill = filler(REST, moe, lambda piece: DveFfn.piece(e, n - 1, piece))

                def pack(*groups):
                    for i in groups if head else ():
                        wait(e, f["hi"], n + 1, i + 1)
                        wait(e, f["tqk"], n + 1, i + 1)
                        e.scalar_tensor_tensor((kp if i % 2 else qp)[:, i // 2, :], hi[:, i % 2, :], mask[:, i % 2:i % 2 + 1], tqk[:, i % 2, :],
                                               ALU.mult, ALU.add).then_inc(f["pack"].sem, 1)

                xc = x_flat[:, bass.ds(c * CH, CH)] if tail else None
                x1c = x1[:].rearrange("p t d -> p (t d)")
                if tail:
                    DveFfn.weigh(e, n, 7)
                fill(1)
                if head:
                    wait(e, f["vps"], n + 1, 1)
                    e.tensor_tensor(vaug[:, :, :, 0:DK], ps[:, 2, :].rearrange("p (t h k) -> p t h k", t=CT, k=DK),
                                    bv_bc[:].rearrange("p (h k) -> p h k", k=DK).unsqueeze(1).broadcast_to([P, CT, HA, DK]), ALU.add).then_inc(f["vaug"].sem, 1)
                if tail:
                    wait(e, f["x1p"], n, 1)
                    wait(e, f["xnb"], n, 1)
                    e.tensor_tensor(x1c, ps[:, 4, :], xn[:].rearrange("p t d -> p (t d)"), ALU.add).then_inc(f["x1"].sem, 1)
                    wait(e, f["x1"], n, 1)
                    norm_stats(e, n, lambda t: x1[:, t, :], st2, mv2, f["stat2"])
                pack(0, 1)
                fill(2)
                if tail:
                    wait(e, f["stat2"], n, 8)
                    wait(e, f["rstd2"], n, 1)
                    for t in range(CT):
                        e.tensor_scalar(o_tm[:, t, :], x1[:, t, :], mv2[:, t, 0:1], r2[:, t:t + 1], ALU.subtract, ALU.mult).then_inc(f["z2"].sem, 1)
                pack(2, 3)
                fill(1)
                if tail:
                    e.scalar_tensor_tensor(xc, x1c, 0.5, xc, ALU.mult, ALU.add).then_inc(f["half"].sem, 1)
                pack(4)
                if tail:
                    DveFfn.choose(e, n)
                fill(2)
                pack(5)
                if tail:
                    DveFfn.route(e, n)
                pack(6, 7)
                if head:
                    DveFfn.residual(e, n + 1, c + 1)
                fill(3)
                if tail:
                    wait(e, f["b2p"], n, 1)
                    wait(e, f["half"], n, 1)
                    e.tensor_tensor(xc, xc, ps[:, 4, :], ALU.add).then_inc(f["acc0"].sem, 1)
                fill(PIECES - REST - 9)
                if tail:
                    wait(e, f["ewn"], n, 1)
                    if moe:
                        wait(e, f["acc"], n - 1, E - 1)
                        wait_alone(e, f["tmp"], n - 1, E)
                    e.tensor_copy(ew[:], ewn[:]).then_inc(f["ew"].sem, 1)

            @staticmethod
            def residual(e, n, c):
                for t in range(CT):
                    e.tensor_scalar(xn[:, t, :], x_flat[:, bass.ds((c * CT + t) * D, D)], mv[:, t, 0:1], r1[:, t:t + 1], ALU.subtract, ALU.mult).then_inc(f["xn"].sem, 1)

            @staticmethod
            def choose(e, n):
                wait(e, f["lgp"], n, 1)
                e.tensor_tensor(lg[:], ps[:, 4, 0:CT * E].rearrange("p (t x) -> p t x", x=E), gb_bc[:].unsqueeze(1).broadcast_to([P, CT, E]), ALU.add).then_inc(f["lg"].sem, 1)
                wait_alone(e, f["lg"], n, 1)
                for t in range(CT):
                    e.max(top[:, t, :], lg[:, t, :]).then_inc(f["top"].sem, 1)
                wait(e, f["top"], n, 4)
                e.tensor_tensor(dv[:], top[:, :, 1], top[:, :, 0], ALU.subtract).then_inc(f["dv"].sem, 1)
                for t in range(CT):
                    e.max_index(tix[:, t, :], top[:, t, :], lg[:, t, :]).then_inc(f["tix"].sem, 1)
                wait(e, f["tix"], n, 4)
                e.tensor_copy(tif[:], tix[:, :, 0:2]).then_inc(f["dv"].sem, 1)

            @staticmethod
            def route(e, n):
                wait(e, f["ev"], n, 1)
                e.tensor_scalar(den[:], ev[:], 2.0, 2.0, ALU.mult, ALU.add).then_inc(f["gw"].sem, 1)
                wait(e, f["gw"], n, 1)
                e.reciprocal(gw1[:], den[:]).then_inc(f["gw"].sem, 1)
                wait(e, f["gw"], n, 2)
                e.tensor_tensor(gw2[:], ev[:], gw1[:], ALU.mult).then_inc(f["gw"].sem, 1)
                wait(e, f["gw"], n, 3)
                wait(e, f["dv"], n, 2)
                for t in range(CT):
                    e.tensor_scalar(ew_a[:, t, :], iota[:], tif[:, t, 0:1], gw1[:, t:t + 1], ALU.is_equal, ALU.mult).then_inc(f["ewab"].sem, 1)
                    e.tensor_scalar(ew_b[:, t, :], iota[:], tif[:, t, 1:2], gw2[:, t:t + 1], ALU.is_equal, ALU.mult).then_inc(f["ewab"].sem, 1)
                wait(e, f["ewab"], n, 8)
                e.tensor_tensor(ewn[:], ew_a[:], ew_b[:], ALU.add).then_inc(f["ewn"].sem, 1)

            @staticmethod
            def experts(e, n, c):
                for piece in range(PIECES):
                    DveFfn.piece(e, n, piece)

        def dve_ret(e, n, c):
            def x_tile(t):
                return x_flat[:, bass.ds((c * CT + t) * D, D)]

            norm_stats(e, n, x_tile, st, mv, r["stat"])
            wait(e, r["stat"], n, 8)
            wait(e, r["rstd"], n, 1)
            for t in range(CT):
                e.tensor_scalar(z[:, t, :], x_tile(t), mv[:, t, 0:1], r1[:, t:t + 1], ALU.subtract, ALU.mult).then_inc(r["z"].sem, 1)
            for i in range(8):
                for k, (table, dst) in enumerate(((cos, ra), (sin, rb))):
                    m = 2 * i + k
                    wait(e, r["qkp"], n, m + 1)
                    if i >= 2:
                        wait(e, r["rot"], n, i - 1)
                    e.tensor_tensor(dst[:, i % 2, :].rearrange("p (b t) -> p b t", b=CB), ps[:, m % 8, :].rearrange("p (b t) -> p b t", b=CB),
                                    table[:].unsqueeze(1).broadcast_to([P, CB, SEQ]), ALU.mult).then_inc(r["rab"].sem, 1)
            for i in range(8):
                wait(e, r["th"], n, i + 1)
                e.scalar_tensor_tensor(sgT[:, i, :], th[:, i % 2, :], 1.0, ps[:, i, :], ALU.add, ALU.mult).then_inc(r["sgT"].sem, 1)

            def group_stats(u):
                b = u % 2
                wait(e, r["op"], n, u + 1)
                if u >= 2:
                    wait(e, r["ors"], n, u - 1)
                for q in range(2):
                    e.bn_stats(ost[:, b, q, :], ps[:, 2 + b, q * P:(q + 1) * P]).then_inc(r["ost"].sem, 1)
                for q in range(2):
                    wait_alone(e, r["ost"], n, 2 * u + q + 1)
                    e.bn_aggr(omv[:, b, q, :], ost[:, b, q, :]).then_inc(r["omv"].sem, 1)

            for u in range(16):
                wait(e, r["scp"], n, u + 1)
                if u >= 2:
                    wait(e, r["op"], n, u - 1)
                e.tensor_tensor(sc[:, u % 2, :], ps[:, u % 2, 0:3 * P], decay[:, u % HR, :], ALU.mult).then_inc(r["sc"].sem, 1)
                if u:
                    group_stats(u - 1)
            group_stats(15)
            wait(e, r["wop"], n, 1)
            xc = x_flat[:, bass.ds(c * CH, CH)]
            e.tensor_tensor(xc, ps[:, 6, :], xc, ALU.add).then_inc(r["x_done"].sem, 1)

        @block.vector
        def _(e):
            e.memset(wqp[:], 0.0).then_inc(spread.sem, 1)
            e.memset(wkp[:], 0.0).then_inc(spread.sem, 1)
            e.memset(bqp[:], 0.0).then_inc(spread.sem, 1)
            e.memset(one1[:], 1.0).then_inc(spread.sem, 1)
            e.wait_ge(spread.sem, 4)
            e.wait_ge(ld["w"], 16 * NLD_W)
            for k, wp in enumerate((wqp, wkp)):
                for part in range(3):
                    e.tensor_copy(wp[:, :, :, part, :], wqkv[:, k * D:(k + 1) * D].rearrange("p (g j k) -> p g j k", g=GA, k=DK)).then_inc(spread.sem, 1)
                    e.tensor_copy(bqp[:, k, :, :, part, :], bqkv[:, k * D:(k + 1) * D].rearrange("p (g j k) -> p g j k", g=GA, k=DK)).then_inc(spread.sem, 1)
            e.memset(bqp[:, 1, :, :, 3, 0:1], 1.0).then_inc(spread.sem, 1)
            e.wait_ge(ld["x"], 16)
            e.wait_ge(zeroed.sem, 4)
            e.wait_ge(vec_sb.sem, 2)
            run_ffn(e, DveFfn, 0)
            e.wait_ge(f["x_done"].sem, NCH)
            e.wait_ge(ld["r"], 16 * NLD_R)
            e.wait_ge(rw_sb.sem, 8)
            src = rw[:, 0:8, :].rearrange("p k (h a d) -> p (k h) a d", a=2, d=32)
            dst = rrot[:].rearrange("p k (h a d) -> p (k h) a d", a=2, d=32)
            e.tensor_scalar(dst[:, :, 0, :], src[:, :, 1, :], -1.0, None, ALU.mult).then_inc(rot_w.sem, 1)
            e.tensor_copy(dst[:, :, 1, :], src[:, :, 0, :]).then_inc(rot_w.sem, 1)
            with e.Fori(0, NCH) as c:
                dve_ret(e, c, c)
            e.wait_ge(r["x_done"].sem, NCH)
            run_ffn(e, DveFfn, 1)

        class ActFfn:
            @staticmethod
            def pre(e, n, c):
                pass

            @staticmethod
            def evac_out(e, n, s):
                wait(e, f["pv"], n, 2 * s + 2)
                if s >= 2:
                    wait(e, f["oqp"], n, s - 1)
                e.activation(ou[:, s % 2, :], ps[:, 4, 0:SEQ], ACT.Identity).then_inc(f["ou"].sem, 1)

            @staticmethod
            def hidden(e, n, piece):
                x, k = divmod(piece, 4)
                if x == E:
                    return
                wait(e, f["zps"], n, piece + 1)
                if k == 0 and x >= 2:
                    wait(e, f["outp"], n, x - 1)
                e.activation(hid[:, x % 2, k, :], ps[:, 6, :], ACT.Relu, bias=vec[:, B1 + piece:B1 + piece + 1]).then_inc(f["hid"].sem, 1)

            @staticmethod
            def steps(e, n, c, moe, ahead):
                fill = filler(0, moe, lambda piece: ActFfn.hidden(e, n - 1, piece))

                def grown(u):
                    wait(e, f["st_ps"], n, u + 1)
                    if u >= 2:
                        wait(e, f["pv"], n, u - 1)
                    e.activation(pt[:, u % 2, :, :], ps[:, 2:4, :], ACT.Exp, scale=float(DK) ** -0.5).then_inc(f["pexp"].sem, 1)

                fill(START)
                for s in range(8):
                    fill(1)
                    grown(2 * s)
                    if s:
                        ActFfn.evac_out(e, n, s - 1)
                    fill(1)
                    grown(2 * s + 1)
                    fill(FILL - 2)
                ActFfn.evac_out(e, n, 7)

            @staticmethod
            def turn(e, n, c, tail, head, moe):
                fill = filler(REST, moe, lambda piece: ActFfn.hidden(e, n - 1, piece))

                def query_key(*groups):
                    for i in groups if head else ():
                        wait(e, f["qkp"], n + 1, i + 1)
                        if i >= 2:
                            wait(e, f["pack"], n + 1, i - 1)
                        e.activation(hi[:, i % 2, :], ps[:, i % 4, :], ACT.Identity, bias=bqk[:, i % 2, i // 2:i // 2 + 1]).then_inc(f["hi"].sem, 1)
                        e.activation(tqk[:, i % 2, :], ps[:, i % 4, :], ACT.Identity, bias=bqk[:, i % 2, i // 2:i // 2 + 1]).then_inc(f["tqk"].sem, 1)

                if head:
                    wait(e, f["hTp"], n + 1, 1)
                    e.activation(hT[:], ps[:, 3, :], ACT.Identity, scale=vec[:, G1:G1 + 1], bias=vec[:, L1B:L1B + 1]).then_inc(f["hT"].sem, 1)
                fill(1)
                if tail:
                    wait(e, f["oTp"], n, 1)
                    e.activation(oT[:], ps[:, 5, :], ACT.Identity).then_inc(f["oT"].sem, 1)
                query_key(0, 1)
                fill(2)
                query_key(2, 3)
                fill(1)
                if tail:
                    wait(e, f["h2Tp"], n, 1)
                    e.activation(h2n[:], ps[:, 5, :], ACT.Identity, scale=vec[:, G2:G2 + 1], bias=vec[:, L2B:L2B + 1]).then_inc(f["h2n"].sem, 1)
                query_key(4)
                fill(1)
                if tail:
                    wait(e, f["dv"], n, 1)
                    e.activation(ev[:], dv[:], ACT.Exp).then_inc(f["ev"].sem, 1)
                fill(1)
                if tail:
                    wait(e, f["h2n"], n, 1)
                    e.activation(h2T[:], h2n[:], ACT.Identity).then_inc(f["h2T"].sem, 1)
                query_key(5, 6, 7)
                if tail:
                    wait(e, f["ewTp"], n, 1)
                    e.activation(ewT[:], ps[0:E, 5, :], ACT.Identity).then_inc(f["ewT"].sem, 1)

            @staticmethod
            def experts(e, n, c):
                for piece in range(PIECES):
                    ActFfn.hidden(e, n, piece)

        def act_ret(e, n):
            wait(e, r["zTp"], n, 1)
            e.activation(zT[:], ps[:, 7, :], ACT.Identity).then_inc(r["zT"].sem, 1)
            for i in range(8):
                wait(e, r["vp"], n, i + 1)
                e.activation(vr[:, i // 2, (i % 2) * 512:(i % 2 + 1) * 512], ps[:, i, :], ACT.Identity).then_inc(r["vr"].sem, 1)
            for i in range(8):
                wait(e, r["gp"], n, i + 1)
                if i >= 2:
                    wait(e, r["sgT"], n, i - 1)
                e.activation(th[:, i % 2, :], ps[:, i, :], ACT.Tanh, scale=0.5).then_inc(r["th"].sem, 1)

            def affine(u):
                h = u % HR
                wait(e, r["ohTp"], n, u + 1)
                if u >= 2:
                    wait(e, r["yT"], n, u - 1)
                e.activation(on[:, u % 2, :], ps[:, 4 + u % 2, 0:SEQ], ACT.Identity, scale=vec[:, GNW + h:GNW + h + 1],
                             bias=vec[:, GNB + h:GNB + h + 1]).then_inc(r["on"].sem, 1)

            for u in range(16):
                b = u % 2
                wait(e, r["ors"], n, u + 1)
                if u >= 2:
                    wait(e, r["ohTp"], n, u - 1)
                for q in range(2):
                    e.activation(oh[:, b, q, :], ps[:, 2 + b, q * P:(q + 1) * P], ACT.Identity, scale=ors[:, b, 1, q:q + 1],
                                 bias=ors[:, b, 3, q:q + 1]).then_inc(r["oh"].sem, 1)
                if u:
                    affine(u - 1)
            affine(15)

        @block.scalar
        def _(e):
            e.wait_ge(vec_ps.sem, 2)
            e.activation(vec[:], ps[:, 0, 0:52], ACT.Identity).then_inc(vec_sb.sem, 1)
            e.activation(bqk[:], ps[:, 1, 0:8].rearrange("p (k g) -> p k g", k=2), ACT.Identity).then_inc(vec_sb.sem, 1)
            e.wait_ge(vec_sb.sem, 2)
            run_ffn(e, ActFfn, 0)
            for i in range(8):
                e.wait_ge(rw_ps.sem, i + 1)
                if i < 6:
                    e.activation(rw[:, 4 * i:4 * i + 4, :], ps[:, i, :].rearrange("p (k o) -> p k o", k=4), ACT.Identity).then_inc(rw_sb.sem, 1)
                else:
                    e.activation(rwo[:, 4 * (i - 6):4 * (i - 6) + 4, :], ps[:, i, :].rearrange("p (k o) -> p k o", k=4), ACT.Identity, scale=0.5).then_inc(rw_sb.sem, 1)
            with e.Fori(0, NCH) as c:
                act_ret(e, c)
            run_ffn(e, ActFfn, 1)

        def transposes(e, dst, src, sig):
            for t in range(CT):
                last = e.transpose(dst(t), src(t), ident[:])
            last.then_inc(sig.sem, 1)

        class PeFfn:
            @staticmethod
            def pre(e, n, c):
                pass

            @staticmethod
            def scores(e, n, s, pr):
                bb, g = divmod(s, GA)
                lo = bb * SEQ
                u = 2 * s + pr
                if u == 0:
                    wait(e, f["pack"], n, 8)
                else:
                    wait(e, f["smax"], n, u)
                for q in range(2):
                    for jj in range(2):
                        j = 32 * (2 * pr + jj)
                        last = e.matmul(ps[:, jj, q * SEQ:(q + 1) * SEQ], qp[j:j + 32, g, lo + q * P:lo + (q + 1) * P],
                                        kp[j:j + 32, g, lo:lo + SEQ], start=True, stop=True)
                last.then_inc(f["s_ps"].sem, 1)

            @staticmethod
            def scores_t(e, n, s, pr):
                bb, g = divmod(s, GA)
                lo = bb * SEQ
                u = 2 * s + pr
                if u:
                    wait(e, f["pexp"], n, u)
                if pr == 0:
                    wait(e, f["qm"], n, s + 1)
                for q in range(2):
                    for jj in range(2):
                        j = 32 * (2 * pr + jj)
                        last = e.matmul(ps[:, 2 + jj, q * SEQ:(q + 1) * SEQ], kp[j:j + 32, g, lo + q * P:lo + (q + 1) * P],
                                        qm[j:j + 32, s % 2, :], start=True, stop=True)
                last.then_inc(f["st_ps"].sem, 1)

            @staticmethod
            def values(e, n, s, pr):
                bb, g = divmod(s, GA)
                u = 2 * s + pr
                if u == 0:
                    wait(e, f["vaug"], n, 1)
                wait(e, f["pexp"], n, u + 1)
                if pr == 0 and s:
                    wait(e, f["ou"], n, s)
                for jj in range(2):
                    j = 2 * pr + jj
                    for k in range(2):
                        last = e.matmul(ps[32 * j:32 * j + 32, 4, 0:SEQ], vaug[:, 2 * bb + k, 4 * g + j, :], pt[:, u % 2, jj, k * SEQ:(k + 1) * SEQ],
                                        start=(k == 0), stop=(k == 1), tile_position=(0, 32 * j))
                last.then_inc(f["pv"].sem, 1)

            @staticmethod
            def out_t(e, n, s):
                wait(e, f["ou"], n, s + 1)
                if s == 7:
                    wait(e, f["o_tm"], n, 7)
                for q in range(2):
                    last = e.transpose(ps[:, 5, q * P:(q + 1) * P], ou[:, s % 2, q * P:(q + 1) * P], ident[:])
                last.then_inc(f["oqp"].sem, 1)

            @staticmethod
            def expert_piece(e, n, piece):
                x, k = divmod(piece, 4)
                if x < E:
                    if piece == 0:
                        wait(e, f["h2T"], n, 1)
                    else:
                        wait(e, f["hid"], n, piece)
                    e.matmul(ps[:, 6, :], w1[:, x, k * P:(k + 1) * P], h2T[:], start=True, stop=True).then_inc(f["zps"].sem, 1)
                if x:
                    if k == 0:
                        wait(e, f["hid"], n, FT * x)
                        if x >= 2:
                            wait(e, f["tmp"], n, x - 1)
                        else:
                            wait(e, f["ew"], n, 1)
                    for i in range(FT):
                        last = e.matmul(ps[:, 7, k * D:(k + 1) * D], hid[:, (x - 1) % 2, i, k * P:(k + 1) * P], w2[:, x - 1, i, :],
                                        start=(i == 0), stop=(i == FT - 1))
                    if k == 3:
                        last.then_inc(f["outp"].sem, 1)

            @staticmethod
            def steps(e, n, c, moe, ahead):
                fill = filler(0, moe, lambda piece: PeFfn.expert_piece(e, n - 1, piece))
                PeFfn.scores(e, n, 0, 0)
                fill(1)
                PeFfn.scores(e, n, 0, 1)
                fill(START - 1)
                for s in range(8):
                    wait(e, f["smax"], n, 2 * s + 2)
                    if s >= 2:
                        wait(e, f["o_tm"], n, s - 1)
                    for q in range(2):
                        last = e.transpose(ps[:, 5, q * P:(q + 1) * P], msp[:, s % 2, q, :], ident[:])
                    last.then_inc(f["mTp"].sem, 1)
                    if s < 7:
                        PeFfn.scores(e, n, s + 1, 0)
                    fill(1)
                    PeFfn.scores_t(e, n, s, 0)
                    if s:
                        PeFfn.values(e, n, s - 1, 1)
                    if s < 7:
                        PeFfn.scores(e, n, s + 1, 1)
                    fill(1)
                    PeFfn.scores_t(e, n, s, 1)
                    fill(FILL - 3)
                    PeFfn.values(e, n, s, 0)
                    if s:
                        PeFfn.out_t(e, n, s - 1)
                    fill(1)
                PeFfn.values(e, n, 7, 1)

            @staticmethod
            def turn(e, n, c, tail, head, moe):
                fill = filler(REST, moe, lambda piece: PeFfn.expert_piece(e, n - 1, piece))

                def query_key(*groups):
                    for i in groups if head else ():
                        if i == 2:
                            wait(e, f["vaug"], n + 1, 1)
                        if i >= 4:
                            wait(e, f["tqk"], n + 1, i - 3)
                        wp = (wkp if i % 2 else wqp)[:, i // 2, :, :, :].rearrange("p j a k -> p (j a k)")
                        e.matmul(ps[:, i % 4, :], wp, hT[:], start=True, stop=True).then_inc(f["qkp"].sem, 1)

                if head:
                    wait(e, f["z"], n + 1, 4)
                    transposes(e, lambda t: ps[:, 3, t * P:(t + 1) * P], lambda t: z[:, t, :], f["hTp"])
                fill(1)
                if tail:
                    PeFfn.out_t(e, n, 7)
                if head:
                    wait(e, f["hT"], n + 1, 1)
                    for t in range(CT):
                        last = e.matmul(ps[:, 2, t * D:(t + 1) * D], hT[:, t * P:(t + 1) * P], wqkv[:, 2 * D:], start=True, stop=True)
                    last.then_inc(f["vps"].sem, 1)
                if tail:
                    wait(e, f["o_tm"], n, 8)
                    transposes(e, lambda t: ps[:, 5, t * P:(t + 1) * P], lambda t: o_tm[:, t, :], f["oTp"])
                query_key(0)
                if tail:
                    wait(e, f["oT"], n, 1)
                    for t in range(CT):
                        last = e.matmul(ps[:, 4, t * D:(t + 1) * D], oT[:, t * P:(t + 1) * P], wo[:], start=True, stop=True)
                    last.then_inc(f["x1p"].sem, 1)
                query_key(1)
                fill(2)
                query_key(2, 3)
                fill(1)
                if tail:
                    wait(e, f["z2"], n, 4)
                    transposes(e, lambda t: ps[:, 5, t * P:(t + 1) * P], lambda t: o_tm[:, t, :], f["h2Tp"])
                query_key(4)
                if tail:
                    wait(e, f["h2n"], n, 1)
                    for t in range(CT):
                        last = e.matmul(ps[:, 4, t * E:(t + 1) * E], h2n[:, t * P:(t + 1) * P], gate_w[:], start=True, stop=True)
                    last.then_inc(f["lgp"].sem, 1)
                fill(2)
                query_key(5)
                fill(1)
                query_key(6)
                fill(1)
                query_key(7)
                if tail:
                    wait(e, f["ewn"], n, 1)
                    for t in range(CT):
                        last = e.transpose(ps[0:E, 5, t * P:(t + 1) * P], ewn[:, t, :], ident[:])
                    last.then_inc(f["ewTp"].sem, 1)
                fill(1)
                if tail:
                    wait(e, f["ewT"], n, 1)
                    e.wait_ge(ld["moe"], 16 * NLD_MOE)
                    for t in range(CT):
                        last = e.matmul(ps[:, 4, t * D:(t + 1) * D], ewT[:, t * P:(t + 1) * P], b2[:], start=True, stop=True)
                    last.then_inc(f["b2p"].sem, 1)
                fill(PIECES - REST - 9)

            @staticmethod
            def experts(e, n, c):
                for piece in range(PIECES):
                    PeFfn.expert_piece(e, n, piece)

        def pe_ret(e, n):
            wait(e, r["z"], n, 4)
            transposes(e, lambda t: ps[:, 7, t * P:(t + 1) * P], lambda t: z[:, t, :], r["zTp"])
            wait(e, r["zT"], n, 1)
            for m in range(16):
                hp, k = divmod(m, 4)
                if m >= 8:
                    wait(e, r["rab"], n, m - 7)
                w = (rrot if k % 2 else rw)[:, hp + 4 * (k // 2), :]
                e.matmul(ps[:, m % 8, :], w, zT[:], start=True, stop=True).then_inc(r["qkp"].sem, 1)
            for i in range(8):
                wait(e, r["rab"], n, 9 + i)
                t, half = divmod(i, 2)
                w = rw[:, 8 + 4 * half:12 + 4 * half, :].rearrange("p k o -> p (k o)")
                e.matmul(ps[:, i, :], zT[:, t * P:(t + 1) * P], w, start=True, stop=True).then_inc(r["vp"].sem, 1)
            for i in range(8):
                wait(e, r["vr"], n, i + 1)
                e.matmul(ps[:, i, :], rw[:, 16 + i, :], zT[:], start=True, stop=True).then_inc(r["gp"].sem, 1)

            def scores(u):
                bb, h = divmod(u, HR)
                j, hp, lo = 64 * (h % 2), h // 2, bb * SEQ
                if u == 0:
                    wait(e, r["rot"], n, 8)
                if u < 2:
                    wait(e, r["sgT"], n, 8)
                else:
                    wait(e, r["sc"], n, u - 1)
                e.matmul(ps[:, u % 2, 0:SEQ], kr[j:j + DR, hp, lo:lo + P], qr[j:j + DR, hp, lo:lo + SEQ], start=True, stop=True)
                e.matmul(ps[:, u % 2, SEQ:SEQ + P], kr[j:j + DR, hp, lo + P:lo + SEQ], qr[j:j + DR, hp, lo + P:lo + SEQ],
                         start=True, stop=True).then_inc(r["scp"].sem, 1)

            def values(u):
                bb, h = divmod(u, HR)
                b = u % 2
                wait(e, r["sc"], n, u + 1)
                if u >= 2:
                    wait(e, r["oh"], n, 2 * u - 2)
                v = [vr[:, 2 * bb + k, h * P:(h + 1) * P] for k in range(2)]
                e.matmul(ps[:, 2 + b, 0:P], sc[:, b, 0:P], v[0], start=True, stop=True)
                e.matmul(ps[:, 2 + b, P:2 * P], sc[:, b, P:2 * P], v[0], start=True, stop=False)
                e.matmul(ps[:, 2 + b, P:2 * P], sc[:, b, 2 * P:3 * P], v[1], start=False, stop=True).then_inc(r["op"].sem, 1)

            def normed_t(u):
                b = u % 2
                wait(e, r["oh"], n, 2 * u + 2)
                if u >= 2:
                    wait(e, r["on"], n, u - 1)
                for q in range(2):
                    last = e.transpose(ps[:, 4 + b, q * P:(q + 1) * P], oh[:, b, q, :], ident[:])
                last.then_inc(r["ohTp"].sem, 1)

            for u in range(18):
                if u < 16:
                    scores(u)
                if 1 <= u <= 16:
                    values(u - 1)
                if u >= 2:
                    normed_t(u - 2)
            wait(e, r["yT"], n, 16)
            for t in range(CT):
                for h in range(HR):
                    last = e.matmul(ps[:, 6, t * D:(t + 1) * D], yT[:, h, t * P:(t + 1) * P], rwo[:, h, :], start=(h == 0), stop=(h == HR - 1))
            last.then_inc(r["wop"].sem, 1)

        @block.tensor
        def _(e):
            e.wait_ge(ld["w"], 16 * NLD_W)
            e.transpose(ps[:, 0, 0:52], vec_rows[:], ident[0:52, 0:52]).then_inc(vec_ps.sem, 1)
            e.wait_ge(spread.sem, 17)
            for k in range(2):
                for g in range(GA):
                    last = e.matmul(ps[:, 1, 4 * k + g:4 * k + g + 1], bqp[:, k, g, :, :, :].rearrange("p j a k -> p (j a k)"), one1[:], start=True, stop=True)
            last.then_inc(vec_ps.sem, 1)
            e.wait_ge(vec_sb.sem, 2)
            e.wait_ge(zeroed.sem, 4)
            run_ffn(e, PeFfn, 0)
            e.wait_ge(ld["r"], 16 * NLD_R)
            e.wait_ge(f["x_done"].sem, NCH)
            for i in range(8):
                for k in range(4):
                    src = ret_in[:, 4 * i + k, :] if i < 6 else wo_in[:, (4 * (i - 6) + k) * P:(4 * (i - 6) + k + 1) * P]
                    last = e.transpose(ps[:, i, k * P:(k + 1) * P], src, ident[:])
                last.then_inc(rw_ps.sem, 1)
            e.wait_ge(rw_sb.sem, 8)
            e.wait_ge(rot_w.sem, 2)
            with e.Fori(0, NCH) as c:
                pe_ret(e, c)
            run_ffn(e, PeFfn, 1)


def kernel(**inputs):
    import concourse.bacc as bacc
    from concourse.bass_utils import run_bass_kernel_spmd as run

    x = np.asarray(inputs["L0_attn_x"])
    nc = bacc.Bacc("TRN2", target_bir_lowering=False, num_devices=1)
    arrays, aps = {}, {}
    for name, v in {**inputs, **constants(x.shape[0] * x.shape[1] // P)}.items():
        v = np.ascontiguousarray(v)
        arrays["in_" + name] = v
        aps[name] = nc.dram_tensor("in_" + name, v.shape, mybir.dt.from_np(v.dtype), kind="ExternalInput").ap()
    out = nc.dram_tensor("out_x", x.shape, F32, kind="ExternalOutput").ap()
    build(nc, aps, out)
    return run(nc, [arrays], core_ids=[0]).results[0]["out_x"]
```

```python
from contextlib import ExitStack

import numpy as np
import concourse.bass as bass
from concourse import mybir

F32 = mybir.dt.float32
F32R = mybir.dt.float32r
U32 = mybir.dt.uint32
ALU = mybir.AluOpType
ACT = mybir.ActivationFunctionType
AX = mybir.AxisListType

P = 128
SEQ = 256
D = 128
CT = 4
CH = CT * P
CB = CH // SEQ
EPS = 1e-5
HA, DK = 16, 8
GA = 4
E, FT = 8, 4
HR, DR = 8, 64
AUG = 24


class Signal:

    def __init__(self, sem, per):
        self.sem, self.per = sem, per

    def __call__(self, n, k):
        return n * self.per + k


def constants(NT):
    inv = (1.0 / np.float32(10000.0) ** (np.arange(0, DR, 2, dtype=np.float32) / np.float32(DR))).astype(np.float32)
    fr = np.arange(SEQ, dtype=np.float32)[:, None] * inv[None, :]
    emb = np.concatenate([fr, fr], -1)
    cos = np.tile(np.cos(emb).T, (2, 1)).astype(np.float32)
    sin = np.tile(np.sin(emb).T * np.where(np.arange(DR) < DR // 2, -1.0, 1.0)[:, None], (2, 1)).astype(np.float32)
    gamma = 1.0 - np.exp2(-5.0 - np.arange(HR, dtype=np.float64))
    s = np.arange(P)[:, None]
    dec = np.zeros((P, HR, 3 * P))
    for h in range(HR):
        rel = np.arange(P)[None, :] - s
        diag = np.where(rel >= 0, gamma[h] ** np.maximum(rel, 0), 0.0)
        dec[:, h, 0:P] = diag
        dec[:, h, P:2 * P] = gamma[h] ** (rel + P)
        dec[:, h, 2 * P:] = diag
    dec *= DR ** -0.5
    mask = np.zeros((P, 2, 2), np.float32)
    for j in range(4):
        mask[32 * j + 16:32 * j + 24, 0, 0] = 1.0
        mask[32 * j + 8:32 * j + 16, 0, 1] = 1.0
    mask[:, 1, :] = 1.0 - 2.0 * mask[:, 0, :]
    return {
        "c_ident": np.eye(P, dtype=np.float32), "c_cos": cos, "c_sin": sin,
        "c_decay": dec.astype(np.float32).reshape(P, HR * 3 * P),
        "c_iota": np.tile(np.arange(E, dtype=np.float32), (P, 1)), "c_mask": mask,
    }


def laid_out(w):
    def strips(v):
        v = v.reshape(-1, GA, 4, 1, DK)
        return np.concatenate([v, v, v, np.zeros_like(v)], 3).reshape(-1, GA * P)

    def tiles(v):
        return v.reshape(-1, P, v.shape[1]).transpose(2, 0, 1)

    qkv, bias = w["L0_ffn_w_qkv"], w["L0_ffn_b_qkv"]
    bqk = np.stack([strips(bias[k * D:(k + 1) * D]).reshape(GA, P).T for k in range(2)], 1)
    bqk[AUG::32, 1, :] = 1.0
    bql = np.zeros_like(bqk)
    for j in range(4):
        for k, row in enumerate((32 * j + 16, 32 * j + 8)):
            bql[row:row + DK, k] = bqk[row:row + DK, k]
    qk = np.concatenate([w["L0_attn_Wq"], w["L0_attn_Wk"]], 0)
    gn = [w["L0_attn_gn_" + k].reshape(HR, P).T for k in ("weight", "bias")]
    ln = [w["L0_ffn_" + k][:, None] for k in ("ln1_g", "ln1_b", "ln2_g", "ln2_b")]
    return {
        "wqp": strips(qkv[:, 0:D]), "wkp": strips(qkv[:, D:2 * D]), "wv": qkv[:, 2 * D:], "bqk": bqk, "bql": bql,
        "vec": np.concatenate([w["L0_ffn_b1"].reshape(E * FT, P).T] + gn + ln, 1),
        "w1": w["L0_ffn_W1"].transpose(1, 0, 2), "w2": w["L0_ffn_W2"].reshape(E, FT, P, D).transpose(2, 0, 1, 3),
        "rw": tiles(qk), "rwvg": tiles(np.concatenate([w["L0_attn_Wv"], w["L0_attn_Wg"]], 0)),
        "rwo": w["L0_attn_Wo"].reshape(D, HR, P).transpose(2, 1, 0),
    }


def build(nc, a, out):
    x_d = a["L0_attn_x"]
    NTOK = x_d.shape[0] * x_d.shape[1]
    NT = NTOK // P
    NCH = NTOK // CH
    ctx = ExitStack()
    scope = [ctx]
    with ctx:
        def sb(name, shape, dt=F32):
            return scope[0].enter_context(nc.sbuf_tensor(name, shape, dt))

        def sg(name, per):
            return Signal(ctx.enter_context(nc.semaphore(name)), per)

        x_sb = sb("x_sb", [P, NT, D])
        w1h = sb("w1h", [P, E, FT * P], F32R)
        w1l = sb("w1l", [P, E, FT * P], F32R)
        w2 = sb("w2", [P, E, FT, D])
        wv = sb("wv", [P, D])
        wqp = sb("wqp", [P, GA, 4, 4, DK])
        wkp = sb("wkp", [P, GA, 4, 4, DK])
        wo = sb("wo", [P, D])
        gate_w = sb("gate_w", [P, E])
        b2 = sb("b2", [E, D])
        bqk = sb("bqk", [P, 2, GA])
        bql = sb("bql", [P, 2, GA])
        bv_bc = sb("bv_bc", [P, D])
        bo_bc = sb("bo_bc", [P, D])
        gb_bc = sb("gb_bc", [P, E])
        vec = sb("vec", [P, 52])
        ident = sb("ident", [P, P])
        cos = sb("cos", [P, SEQ])
        sin = sb("sin", [P, SEQ])
        decay = sb("decay", [P, HR, 3 * P])
        iota = sb("iota", [P, E])
        mask = sb("mask", [P, 2, 2])
        rw = sb("rw", [P, 8, P])
        rwh = sb("rwh", [P, 16, P], F32R)
        split = ExitStack()
        rw_in = split.enter_context(nc.sbuf_tensor("rw_in", [P, 16, P], F32))
        split.close()
        rwl = sb("rwl", [P, 16, P], F32R)
        rwo = sb("rwo", [P, HR, D])
        mhalf = sb("mhalf", [P, CT])
        B1, GNW, GNB, G1, L1B, G2, L2B = 0, 32, 40, 48, 49, 50, 51

        vaug = sb("vaug", [P, CT, HA, 32])
        msp = sb("msp", [P, 2, 2, P])
        ln_t = sb("ln_t", [P, 6, CT])
        st = sb("st", [P, CT, 6])
        mv = sb("mv", [P, CT, 2])
        r1 = sb("r1", [P, CT])
        r12 = sb("r12", [P, CT])
        z = sb("z", [P, CT, D])
        ffn_only = ExitStack()
        scope[0] = ffn_only
        h2h = sb("h2h", [P, CH], F32R)
        h2l = sb("h2l", [P, CH], F32R)
        hid = sb("hid", [P, 2, FT, CH])
        tmp = sb("tmp", [P, 2, CH])
        ew = sb("ew", [P, CT, E])
        xn = sb("xn", [P, CT, D])
        hT = sb("hT", [P, CH])
        tqk = sb("tqk", [P, 2, CH])
        hi = sb("hi", [P, 2, CH], F32R)
        qp = sb("qp", [P, GA, CH], F32R)
        kp = sb("kp", [P, GA, CH], F32R)
        qm = sb("qm", [P, 2, SEQ], F32R)
        pt = sb("pt", [P, 2, 2, 2 * SEQ])
        ou = sb("ou", [P, 2, SEQ])
        rec = sb("rec", [P, 2, 2, 4])
        o_tm = sb("o_tm", [P, CT, D])
        oT = sb("oT", [P, CH])
        x1 = sb("x1", [P, CT, D])
        st2 = sb("st2", [P, CT, 6])
        mv2 = sb("mv2", [P, CT, 2])
        r2 = sb("r2", [P, CT])
        h2n = sb("h2n", [P, CH])
        ewT = sb("ewT", [E, CH])
        lg = sb("lg", [P, CT, E])
        top = sb("top", [P, CT, 8])
        tix = sb("tix", [P, CT, 8], U32)
        tif = sb("tif", [P, CT, 2])
        dv = sb("dv", [P, CT])
        ev = sb("ev", [P, CT])
        den = sb("den", [P, CT])
        gw1 = sb("gw1", [P, CT])
        gw2 = sb("gw2", [P, CT])
        ew_a = sb("ew_a", [P, CT, E])
        ew_b = sb("ew_b", [P, CT, E])
        ewn = sb("ewn", [P, CT, E])
        ffn_only.close()
        scope[0] = ctx
        yT = sb("yT", [P, 2, HR, SEQ])
        sc = sb("sc", [P, 2, 3 * P])
        ost = sb("ost", [P, 2, 2, 6])
        omv = sb("omv", [P, 2, 2, 2])
        ors = sb("ors", [P, 2, 3, 2])
        oh = sb("oh", [P, 2, 2, P])
        on = sb("on", [P, 2, SEQ])
        sg1 = sb("sg1", [P, HR, SEQ])
        zT = sb("zT", [P, SEQ])
        zh = sb("zh", [P, SEQ], F32R)
        zl = sb("zl", [P, SEQ], F32R)
        th = sb("th", [P, 2, 2 * SEQ])
        qkr = [sb("qr", [P, 2, 4, SEQ]), sb("kr", [P, 2, 4, SEQ])]
        swap = sb("swap", [P, 2, 4, SEQ])
        vr = sb("vr", [P, 2, 2, HR * P])
        sgT = [sb("sg0", [P, HR, SEQ]), sg1]

        ps = ctx.enter_context(nc.psum_tensor("ps", [P, 8, 512], F32))

        ld = {k: ctx.enter_context(nc.semaphore("ld_" + k)) for k in ("x0", "x", "w", "late", "moe", "r")}
        zeroed = sg("zeroed", 0)
        w1_high = sg("w1_high", 0)
        w1_low = sg("w1_low", 0)
        rw_high = sg("rw_high", 0)
        rw_low = sg("rw_low", 0)
        f = {k: sg("f_" + k, v) for k, v in dict(
            stat=8, rstd=1, xn=4, z=4, xnb=1, hTp=1, hT=1, qkp=8, tqk=8, hi=8, pack=8, vps=1, vaug=1,
            s_ps=16, smax=16, mTp=8, qm=8, st_ps=16, pexp=16, pv=16, ou=8, oqp=8, rec=8, o_tm=8, oTp=1, oT=1,
            x1p=1, x1=1, stat2=8, rstd2=1, z2=4, h2Tp=1, h2n=1, h2h=1, h2l=1, lgp=1, lg=1, top=4, tix=4, dv=2, ev=1, gw=3, ewab=4,
            ewn=1, ew=1, ewTp=1, ewT=1, half=1, b2p=1, acc0=1, zps=32, hid=32, outp=8, tmp=8, acc=7, x_done=1, chain=6, chain2=1).items()}
        r = {k: sg("r_" + k, v) for k, v in dict(
            stat=8, rstd=1, z=4, chain_z=1).items()}
        r.update({k: sg("r_" + k, v) for k, v in dict(
            zTp=1, zT=1, zh=1, zl=1, qkp=4, qk=4, swap_q=64, swap_k=64, swap_sin=4, cos=4, rot=4, vp=4, vr=4, gp=4, th=4, sgT=4, scp=8, sc=8, op=8, ost=16, omv=16,
            chain=8, ors=8, shift=8, oh=16, ohTp=8, on=8, yT=8, wop=1, x_done=1).items()})
        swapped = r["swap_q"], r["swap_k"]
        stored = ctx.enter_context(nc.semaphore("stored"))
        passed = ctx.enter_context(nc.semaphore("passed"))
        x_flat = x_sb[:].rearrange("p n d -> p (n d)")
        x_tok = x_d.rearrange("b (t p) d -> p (b t) d", p=P)
        w1_in = hid[:].rearrange("p b k t -> p (b k t)")
        out_tok = out.rearrange("b (t p) d -> p (b t) d", p=P)
        NLD_W, NLD_LATE, NLD_MOE, NLD_R = 9, 6, 3, 5

        block = ctx.enter_context(nc.Block())

        def run_ffn(e, eng, rnd):
            n0 = rnd * NCH
            if rnd == 0:
                eng.pre(e, n0, 0)
            eng.turn(e, n0 - 1, -1, False, True, False)
            eng.steps(e, n0, 0, False, True)
            eng.turn(e, n0, 0, True, True, False)
            with e.Fori(1, NCH - 1) as c:
                eng.steps(e, c + n0, c, True, True)
                eng.turn(e, c + n0, c, True, True, True)
            last = n0 + NCH - 1
            eng.steps(e, last, NCH - 1, True, False)
            eng.turn(e, last, NCH - 1, True, False, True)

        def run(e, ffn, ret):
            run_ffn(e, ffn, 0)
            start_ret(e, ret)
            ffn.experts(e, NCH - 1, NCH - 1)
            run_ret(e, ret)
            run_ffn(e, ffn, 1)
            ffn.experts(e, 2 * NCH - 1, NCH - 1)

        PIECES = 4 * (E + 1)
        START, FILL = 4, 3
        REST = START + 8 * FILL

        def filler(first, on, do):
            piece = first

            def fill(many):
                nonlocal piece
                for _ in range(many if on else 0):
                    do(piece)
                    piece += 1
            return fill

        def score_banks(u, moe):
            return slice(0, 2) if moe or (u >= 2 and u % 2 == 0) else slice(6, 8)

        def hidden_bank(piece, alone):
            return 0 if alone and piece % 2 else 6

        def out_bank(x, alone):
            return 1 if alone and x % 2 else 7

        def finishes(piece):
            return piece >= 4 and piece % 4 == 3

        PROJ, OUT = 13, (13, 14)
        SIN, ADD = (15, 16, 17, 18), (19, 20, 21, 22)
        SILU = (23, 24, 25, 26)
        PLAN = (((0,), (1,)), ((2,), (3,)), ((4,), (5,)), ((SILU[0], 6), (SIN[0], SILU[1])),
                ((7, SIN[1]), (OUT[0], SIN[2])), ((8, SILU[2], SIN[3]), (OUT[1], ADD[0])),
                ((SILU[3], 9, ADD[1]), (10, ADD[2])), ((11, ADD[3]), (12,)))
        FIRST = (*range(7), SILU[0], 7, SILU[1], 8, SILU[2], 9, SILU[3], 10, 11, 12, *SIN, *ADD)
        LAG = 4

        def start_ret(e, eng):
            for p in FIRST:
                eng.piece(e, 0, 0, 0, p, 2)

        def run_ret(e, eng):
            eng.steps(e, 0, range(2 * HR), False, True)
            with e.Fori(1, NCH - 1) as c:
                eng.steps(e, c, range(2 * HR), True, True)
            eng.steps(e, NCH - 1, range(2 * HR + LAG), True, False)
            for p in OUT:
                eng.piece(e, 2 * NCH - 1, NCH - 1, 1, p)

        def planned(e, eng, c, u, gap, before, after):
            for p in PLAN[u % HR][gap] if u < 2 * HR else ():
                half = u // HR
                if p not in OUT and (half == 0 or after):
                    eng.piece(e, 2 * c + 1 + half, c + half, 1 - half, p)
                if p in OUT and (half == 1 or before):
                    eng.piece(e, 2 * c - 1 + half, c - 1 + half, 1 - half, p)

        def on_way(u, before):
            return u < 2 * HR and (u >= 0 or before)

        def wait_earlier(e, sig, n, k):
            count = sig(n, k)
            if not (isinstance(count, int) and count <= 0):
                e.wait_ge(sig.sem, count)


        class SpRet:
            @staticmethod
            def piece(e, s, c, bb, p, base=6):
                if p in (2, 4):
                    b = p // 2 - 1
                    e.wait_ge(r["qk"].sem, r["qk"](s, p))
                    for i in range(4):
                        lo, other = i * DR // 2, (i ^ 1) * DR // 2
                        e.dma_start(swap[lo:lo + DR // 2, b, :, :], qkr[b][other:other + DR // 2, bb, :, :]).then_inc(swapped[b].sem, 16)

            @staticmethod
            def steps(e, c, steps, before, after):
                for u in steps:
                    for gap in range(2):
                        planned(e, SpRet, c, u, gap, before, after)

        @block.sync
        def _(e):
            e.dma_start(x_sb[:, 0:CT, :], x_tok[:, 0:CT, :]).then_inc(ld["x0"], 16)
            for dst, src in (
                (ident[:], a["c_ident"]), (vec[:], a["vec"]), (wv[:], a["wv"]), (bqk[:], a["bqk"]), (bql[:], a["bql"]),
                (wqp[:].rearrange("p g j a k -> p (g j a k)"), a["wqp"]), (wkp[:].rearrange("p g j a k -> p (g j a k)"), a["wkp"]),
                (bv_bc[:], a["L0_ffn_b_qkv"][2 * D:3 * D].partition_broadcast(P)), (mask[:], a["c_mask"]),
            ):
                e.dma_start(dst, src).then_inc(ld["w"], 16)
            e.dma_start(x_sb[:, CT:, :], x_tok[:, CT:, :]).then_inc(ld["x"], 16)
            for dst, src in (
                (iota[:], a["c_iota"]), (wo[:], a["L0_ffn_w_o"]), (gate_w[:], a["L0_ffn_gate_w"]),
                (bo_bc[:], a["L0_ffn_b_o"].partition_broadcast(P)), (gb_bc[:], a["L0_ffn_gate_b"].partition_broadcast(P)),
                (b2[:], a["L0_ffn_b2"]),
            ):
                e.dma_start(dst, src).then_inc(ld["late"], 16)
            e.dma_start(w1_in, a["w1"].rearrange("p x f -> p (x f)")).then_inc(ld["moe"], 16)
            e.dma_start(w2[:], a["w2"]).then_inc(ld["moe"], 16)
            e.dma_start(rw_in[:], a["rwvg"]).then_inc(ld["moe"], 16)
            e.dma_start(rw[:], a["rw"]).then_inc(ld["r"], 16)
            e.dma_start(rwo[:], a["rwo"]).then_inc(ld["r"], 16)
            e.dma_start(decay[:], a["c_decay"].rearrange("p (h k) -> p h k", h=HR)).then_inc(ld["r"], 16)
            e.dma_start(cos[:], a["c_cos"]).then_inc(ld["r"], 16)
            e.dma_start(sin[:], a["c_sin"]).then_inc(ld["r"], 16)
            start_ret(e, SpRet)
            run_ret(e, SpRet)
            with e.Fori(0, NCH) as c:
                e.wait_ge(f["x_done"].sem, f["x_done"](c + NCH, 1))
                e.dma_start(out_tok[:, bass.ds(c * CT, CT), :], x_sb[:, bass.ds(c * CT, CT), :]).then_inc(stored, 16)
            e.wait_ge(stored, 16 * NCH)

        class PoolFfn:
            @staticmethod
            def pre(e, n, c):
                e.wait_ge(f["stat"].sem, f["stat"](n, 8))
                e.sem_inc(passed)
                e.tensor_scalar(ln_t[:, 0, :], mv[:, :, 1], 1.0, EPS, ALU.mult, ALU.add).then_inc(f["chain"].sem, 1)
                e.wait_ge(f["chain"].sem, f["chain"](n, 1))
                e.sem_inc(passed)
                e.tensor_tensor(r1[:], ln_t[:, 0, :], mhalf[:], ALU.pow).then_inc(f["chain"].sem, 1)
                e.wait_ge(f["chain"].sem, f["chain"](n, 2))
                e.sem_inc(passed)
                e.tensor_tensor(ln_t[:, 1, :], r1[:], r1[:], ALU.mult).then_inc(f["chain"].sem, 1)
                e.wait_ge(f["chain"].sem, f["chain"](n, 3))
                e.sem_inc(passed)
                e.tensor_tensor(ln_t[:, 2, :], ln_t[:, 1, :], mv[:, :, 1], ALU.mult).then_inc(f["chain"].sem, 1)
                e.wait_ge(f["chain"].sem, f["chain"](n, 4))
                e.sem_inc(passed)
                e.tensor_scalar(ln_t[:, 3, :], ln_t[:, 2, :], 1.0, EPS, ALU.mult, ALU.add).then_inc(f["chain"].sem, 1)
                e.wait_ge(f["chain"].sem, f["chain"](n, 5))
                e.sem_inc(passed)
                e.tensor_tensor(ln_t[:, 4, :], ln_t[:, 3, :], mhalf[:], ALU.pow).then_inc(f["chain"].sem, 1)
                e.wait_ge(f["chain"].sem, f["chain"](n, 6))
                e.sem_inc(passed)
                e.tensor_tensor(r12[:], r1[:], ln_t[:, 4, :], ALU.mult).then_inc(f["rstd"].sem, 1)

            @staticmethod
            def turn(e, n, c, tail, head, moe):
                fill = filler(REST, moe, lambda piece: PoolFfn.piece(e, n - 1, c - 1, piece))
                fill(3)
                if tail:
                    e.wait_ge(f["stat2"].sem, f["stat2"](n, 8))
                    e.sem_inc(passed)
                    e.tensor_scalar(ln_t[:, 5, :], mv2[:, :, 1], 1.0, EPS, ALU.mult, ALU.add).then_inc(f["chain2"].sem, 1)
                    e.wait_ge(f["chain2"].sem, f["chain2"](n, 1))
                    e.sem_inc(passed)
                    e.tensor_tensor(r2[:], ln_t[:, 5, :], mhalf[:], ALU.pow).then_inc(f["rstd2"].sem, 1)
                fill(PIECES - REST - 3)

            @staticmethod
            def piece(e, n, c, piece):
                if not finishes(piece):
                    return
                x = piece // 4 - 1
                e.wait_ge(f["tmp"].sem, f["tmp"](n, x + 1))
                before = f["acc"] if x else f["acc0"]
                e.wait_ge(before.sem, before(n, x or 1))
                e.sem_inc(passed)
                xc = x_flat[:, bass.ds(c * CH, CH)]
                e.tensor_tensor(xc, xc, tmp[:, x % 2, :], ALU.add).then_inc((f["acc"] if x < E - 1 else f["x_done"]).sem, 1)

            @staticmethod
            def steps(e, n, c, moe, ahead):
                fill = filler(0, moe, lambda piece: PoolFfn.piece(e, n - 1, c - 1, piece))
                fill(START + FILL)
                if not moe:
                    e.wait_ge(ld["late"], 16 * NLD_LATE)
                e.wait_ge(f["xn"].sem, f["xn"](n, 4))
                e.tensor_tensor(xn[:], xn[:], bo_bc[:].unsqueeze(1).broadcast_to([P, CT, D]), ALU.add).then_inc(f["xnb"].sem, 1)
                fill(4 * FILL)
                if ahead:
                    PoolFfn.pre(e, n + 1, c + 1)
                elif n < NCH:
                    PoolRet.norm(e, 0)
                fill(3 * FILL)

            @staticmethod
            def experts(e, n, c):
                for piece in range(PIECES):
                    PoolFfn.piece(e, n, c, piece)

        class PoolRet:
            @staticmethod
            def norm(e, c):
                e.wait_ge(r["stat"].sem, r["stat"](c, 8))
                e.sem_inc(passed)
                e.tensor_scalar(ln_t[:, 0, :], mv[:, :, 1], 1.0, EPS, ALU.mult, ALU.add).then_inc(r["chain_z"].sem, 1)
                e.wait_ge(r["chain_z"].sem, r["chain_z"](c, 1))
                e.sem_inc(passed)
                e.tensor_tensor(r1[:], ln_t[:, 0, :], mhalf[:], ALU.pow).then_inc(r["rstd"].sem, 1)

            @staticmethod
            def piece(e, s, c, bb, p, base=6):
                if p in SIN:
                    b, i = divmod(SIN.index(p), 2)
                    part = qkr[b][:, bb, 2 * i:2 * i + 2, :]
                    e.wait_ge(swapped[b].sem, swapped[b](s, 64))
                    e.tensor_tensor(part, part, cos[:].unsqueeze(1).broadcast_to([P, 2, SEQ]), ALU.mult).then_inc(r["cos"].sem, 1)

            @staticmethod
            def steps(e, c, steps, before, after):
                def group_rstd(u):
                    b = u % 2
                    wait_earlier(e, r["oh"], 2 * c, 2 * u - 2)
                    e.wait_ge(r["omv"].sem, r["omv"](2 * c, 2 * u + 2))
                    e.sem_inc(passed)
                    e.tensor_scalar(ors[:, b, 0, :], omv[:, b, :, 1], 1.0, EPS, ALU.mult, ALU.add).then_inc(r["chain"].sem, 1)
                    e.wait_ge(r["chain"].sem, r["chain"](2 * c, u + 1))
                    e.sem_inc(passed)
                    e.tensor_tensor(ors[:, b, 1, :], ors[:, b, 0, :], mhalf[:, 0:2], ALU.pow).then_inc(r["ors"].sem, 1)

                def gate(u):
                    h, bb = u % HR, u // HR % 2
                    e.wait_ge(r["on"].sem, r["on"](2 * c, u + 1))
                    if h == 0:
                        e.wait_ge(r["sgT"].sem, r["sgT"](2 * c, 4 * (u // HR) + 4))
                    e.tensor_tensor(yT[:, bb, h, :], on[:, u % 2, :], sgT[bb][:, h, :], ALU.mult).then_inc(r["yT"].sem, 1)

                for u in steps:
                    if on_way(u - 4, before):
                        gate(u - 4)
                    planned(e, PoolRet, c, u, 0, before, after)
                    if on_way(u - 1, before):
                        group_rstd(u - 1)
                    planned(e, PoolRet, c, u, 1, before, after)
                    if u == 3 and after:
                        PoolRet.norm(e, c + 1)
                    if u == 3 and not after:
                        PoolFfn.pre(e, NCH, 0)

        @block.gpsimd
        def _(e):
            e.memset(mhalf[:], -0.5).then_inc(zeroed.sem, 1)
            e.memset(vaug[:], 0.0).then_inc(zeroed.sem, 1)
            e.memset(msp[:], 0.0).then_inc(zeroed.sem, 1)
            e.wait_ge(zeroed.sem, 3)
            e.memset(vaug[:, :, :, DK:DK + 1], 1.0).then_inc(zeroed.sem, 1)
            run(e, PoolFfn, PoolRet)

        def norm_stats(e, n, src, s_, m_, sig):
            for t in range(CT):
                e.bn_stats(s_[:, t, :], src(t)).then_inc(sig.sem, 1)
            for t in range(CT):
                e.wait_ge(sig.sem, sig(n, t + 1))
                e.sem_inc(passed)
                e.bn_aggr(m_[:, t, :], s_[:, t, :]).then_inc(sig.sem, 1)

        class DveFfn:
            @staticmethod
            def stats(e, n, c):
                norm_stats(e, n, lambda t: x_flat[:, bass.ds((c * CT + t) * D, D)], st, mv, f["stat"])

            @staticmethod
            def rows(e, n, c):
                e.wait_ge(f["stat"].sem, f["stat"](n, 8))
                e.wait_ge(f["rstd"].sem, f["rstd"](n, 1))
                for t in range(CT):
                    e.tensor_scalar(z[:, t, :], x_flat[:, bass.ds((c * CT + t) * D, D)], mv[:, t, 0:1], r12[:, t:t + 1],
                                    ALU.subtract, ALU.mult).then_inc(f["z"].sem, 1)

            @staticmethod
            def pre(e, n, c):
                DveFfn.stats(e, n, c)
                DveFfn.rows(e, n, c)

            @staticmethod
            def pack(e, n, i):
                e.wait_ge(f["hi"].sem, f["hi"](n, i + 1))
                e.wait_ge(f["tqk"].sem, f["tqk"](n, i + 1))
                e.scalar_tensor_tensor((kp if i % 2 else qp)[:, i // 2, :], hi[:, i % 2, :], mask[:, 1, i % 2:i % 2 + 1], tqk[:, i % 2, :],
                                       ALU.mult, ALU.add).then_inc(f["pack"].sem, 1)

            @staticmethod
            def value_rows(e, n, bank):
                e.wait_ge(f["vps"].sem, f["vps"](n, 1))
                e.tensor_tensor(vaug[:, :, :, 0:DK], ps[:, bank, :].rearrange("p (t h k) -> p t h k", t=CT, k=DK),
                                bv_bc[:].rearrange("p (h k) -> p h k", k=DK).unsqueeze(1).broadcast_to([P, CT, HA, DK]), ALU.add).then_inc(f["vaug"].sem, 1)

            @staticmethod
            def weigh(e, n, s):
                bb, g = divmod(s, GA)
                e.wait_ge(f["oqp"].sem, f["oqp"](n, s + 1))
                o = ps[:, 5, 0:SEQ].rearrange("p (q j k) -> p q j k", q=2, k=32)
                e.reciprocal(rec[:, s % 2, :, :], o[:, :, :, DK]).then_inc(f["rec"].sem, 1)
                e.wait_ge(f["rec"].sem, f["rec"](n, s + 1))
                e.tensor_tensor(o_tm[:, 2 * bb:2 * bb + 2, 32 * g:32 * g + 32].rearrange("p q (j k) -> p q j k", k=DK), o[:, :, :, 0:DK],
                                rec[:, s % 2, :, :].unsqueeze(3).broadcast_to([P, 2, 4, DK]), ALU.mult).then_inc(f["o_tm"].sem, 1)

            @staticmethod
            def biggest(e, n, s, pr, moe):
                e.wait_ge(f["s_ps"].sem, f["s_ps"](n, 2 * s + pr + 1))
                e.tensor_reduce(msp[:, s % 2, :, 64 * pr + AUG:64 * pr + AUG + 33:32].rearrange("p q j -> p j q"),
                                ps[:, score_banks(2 * s + pr, moe), :].rearrange("p j (q k) -> p j q k", q=2), AX.X, ALU.max, negate=True).then_inc(f["smax"].sem, 1)

            @staticmethod
            def piece(e, n, piece, alone=False):
                if not finishes(piece):
                    return
                x = piece // 4 - 1
                e.wait_ge(f["outp"].sem, f["outp"](n, x + 1))
                if x == 0:
                    e.wait_ge(f["ew"].sem, f["ew"](n, 1))
                if x:
                    e.wait_ge(f["acc"].sem, f["acc"](n, max(x - 1, 1)))
                e.tensor_tensor(tmp[:, x % 2, :].rearrange("p (t d) -> p t d", d=D), ps[:, out_bank(x, alone), :].rearrange("p (t d) -> p t d", d=D),
                                ew[:, :, x:x + 1].broadcast_to([P, CT, D]), ALU.mult).then_inc(f["tmp"].sem, 1)

            @staticmethod
            def steps(e, n, c, moe, ahead):
                fill = filler(0, moe, lambda piece: DveFfn.piece(e, n - 1, piece))
                if not moe:
                    e.wait_ge(ld["x"], 16)
                if not moe:
                    DveFfn.biggest(e, n, 0, 0, moe)
                if moe:
                    DveFfn.route(e, n - 1)
                    DveFfn.weights(e, n - 1)
                if not moe:
                    DveFfn.pack(e, n, 3)
                    DveFfn.pack(e, n, 4)
                DveFfn.biggest(e, n, 0, 1, moe)
                if not moe:
                    DveFfn.pack(e, n, 5)
                fill(START)
                if moe:
                    DveFfn.bias(e, n - 1, c - 1)
                for s in range(8):
                    bb, g = divmod(s, GA)
                    e.wait_ge(f["mTp"].sem, f["mTp"](n, s + 1))
                    e.tensor_tensor(qm[:, s % 2, :], ps[:, 5, 0:SEQ], qp[:, g, bb * SEQ:(bb + 1) * SEQ].bitcast(F32), ALU.add).then_inc(f["qm"].sem, 1)
                    if s < 7:
                        DveFfn.biggest(e, n, s + 1, 0, moe)
                    fill(1)
                    if s == 0 and not moe:
                        DveFfn.value_rows(e, n, 4)
                    if s < 7:
                        DveFfn.biggest(e, n, s + 1, 1, moe)
                    fill(1)
                    if s == 1 and not moe:
                        DveFfn.pack(e, n, 6)
                        DveFfn.pack(e, n, 7)
                    if s == 0:
                        DveFfn.residual(e, n, c)
                    if ahead and s == 4:
                        DveFfn.stats(e, n + 1, c + 1)
                    if ahead and s == 6:
                        DveFfn.rows(e, n + 1, c + 1)
                    if not ahead and n < NCH:
                        if s == 4:
                            DveRet.stats(e, 0)
                        if s == 6:
                            DveRet.rows(e, 0)
                    if s:
                        DveFfn.weigh(e, n, s - 1)
                    fill(FILL - 2)
                    if not moe and n == 0 and s:
                        DveFfn.split_low(e, s - 1)
                if not moe and n == 0:
                    DveFfn.split_low(e, 7)

            @staticmethod
            def split_low(e, s):
                e.wait_ge(w1_high.sem, s + 1)
                e.tensor_tensor(w1l[:, s, :], w1_in[:, s * FT * P:(s + 1) * FT * P], w1h[:, s, :].bitcast(F32), ALU.subtract).then_inc(w1_low.sem, 1)
                e.wait_ge(rw_high.sem, s + 1)
                e.tensor_tensor(rwl[:, 2 * s:2 * s + 2, :], rw_in[:, 2 * s:2 * s + 2, :], rwh[:, 2 * s:2 * s + 2, :].bitcast(F32), ALU.subtract).then_inc(rw_low.sem, 1)

            @staticmethod
            def turn(e, n, c, tail, head, moe):
                fill = filler(REST, moe, lambda piece: DveFfn.piece(e, n - 1, piece))

                def pack(*groups):
                    for i in groups if head else ():
                        DveFfn.pack(e, n + 1, i)

                if not tail:
                    e.wait_ge(ld["w"], 16 * NLD_W)
                    e.wait_ge(zeroed.sem, 4)
                xc = x_flat[:, bass.ds(c * CH, CH)] if tail else None
                x1c = x1[:].rearrange("p t d -> p (t d)")
                if tail:
                    DveFfn.weigh(e, n, 7)
                fill(1)
                if head and tail:
                    DveFfn.value_rows(e, n + 1, 2)
                if tail:
                    e.wait_ge(f["x1p"].sem, f["x1p"](n, 1))
                    e.wait_ge(f["xnb"].sem, f["xnb"](n, 1))
                    e.tensor_tensor(x1c, ps[:, 4, :], xn[:].rearrange("p t d -> p (t d)"), ALU.add).then_inc(f["x1"].sem, 1)
                    e.wait_ge(f["x1"].sem, f["x1"](n, 1))
                    norm_stats(e, n, lambda t: x1[:, t, :], st2, mv2, f["stat2"])
                pack(0, 1)
                fill(2)
                if tail:
                    e.wait_ge(f["stat2"].sem, f["stat2"](n, 8))
                    e.wait_ge(f["rstd2"].sem, f["rstd2"](n, 1))
                    for t in range(CT):
                        e.tensor_scalar(o_tm[:, t, :], x1[:, t, :], mv2[:, t, 0:1], r2[:, t:t + 1], ALU.subtract, ALU.mult).then_inc(f["z2"].sem, 1)
                pack(2)
                if not tail:
                    return
                pack(3)
                fill(1)
                if tail:
                    e.scalar_tensor_tensor(xc, x1c, 0.5, xc, ALU.mult, ALU.add).then_inc(f["half"].sem, 1)
                pack(4)
                if tail:
                    DveFfn.choose(e, n)
                pack(5)
                fill(2)
                if tail:
                    e.wait_ge(f["h2h"].sem, f["h2h"](n, 1))
                    e.tensor_tensor(h2l[:], h2n[:], h2h[:].bitcast(F32), ALU.subtract).then_inc(f["h2l"].sem, 1)
                pack(6, 7)
                if not head:
                    DveFfn.route(e, n)
                if head:
                    DveFfn.biggest(e, n + 1, 0, 0, True)
                fill(PIECES - REST - 6)
                if not head:
                    DveFfn.bias(e, n, c)
                if moe:
                    e.wait_ge(f["acc"].sem, f["acc"](n - 1, E - 1))
                    e.wait_ge(f["tmp"].sem, f["tmp"](n - 1, E))
                    e.sem_inc(passed)
                if not head:
                    DveFfn.weights(e, n)

            @staticmethod
            def weights(e, n):
                e.wait_ge(f["ewn"].sem, f["ewn"](n, 1))
                e.sem_inc(passed)
                e.tensor_copy(ew[:], ewn[:]).then_inc(f["ew"].sem, 1)

            @staticmethod
            def bias(e, n, c):
                xc = x_flat[:, bass.ds(c * CH, CH)]
                e.wait_ge(f["b2p"].sem, f["b2p"](n, 1))
                e.wait_ge(f["half"].sem, f["half"](n, 1))
                e.tensor_tensor(xc, xc, ps[:, 4, :], ALU.add).then_inc(f["acc0"].sem, 1)

            @staticmethod
            def residual(e, n, c):
                for t in range(CT):
                    e.tensor_scalar(xn[:, t, :], x_flat[:, bass.ds((c * CT + t) * D, D)], mv[:, t, 0:1], r1[:, t:t + 1], ALU.subtract, ALU.mult).then_inc(f["xn"].sem, 1)

            @staticmethod
            def choose(e, n):
                e.wait_ge(ld["late"], 16 * NLD_LATE)
                e.wait_ge(f["lgp"].sem, f["lgp"](n, 1))
                e.tensor_tensor(lg[:], ps[:, 4, 0:CT * E].rearrange("p (t x) -> p t x", x=E), gb_bc[:].unsqueeze(1).broadcast_to([P, CT, E]), ALU.add).then_inc(f["lg"].sem, 1)
                e.wait_ge(f["lg"].sem, f["lg"](n, 1))
                e.sem_inc(passed)
                for t in range(CT):
                    e.max(top[:, t, :], lg[:, t, :]).then_inc(f["top"].sem, 1)
                e.wait_ge(f["top"].sem, f["top"](n, 4))
                e.tensor_tensor(dv[:], top[:, :, 1], top[:, :, 0], ALU.subtract).then_inc(f["dv"].sem, 1)
                for t in range(CT):
                    e.max_index(tix[:, t, :], top[:, t, :], lg[:, t, :]).then_inc(f["tix"].sem, 1)
                e.wait_ge(f["tix"].sem, f["tix"](n, 4))
                e.tensor_copy(tif[:], tix[:, :, 0:2]).then_inc(f["dv"].sem, 1)

            @staticmethod
            def route(e, n):
                e.wait_ge(f["ev"].sem, f["ev"](n, 1))
                e.tensor_scalar(den[:], ev[:], 2.0, 2.0, ALU.mult, ALU.add).then_inc(f["gw"].sem, 1)
                e.wait_ge(f["gw"].sem, f["gw"](n, 1))
                e.reciprocal(gw1[:], den[:]).then_inc(f["gw"].sem, 1)
                e.wait_ge(f["gw"].sem, f["gw"](n, 2))
                e.tensor_tensor(gw2[:], ev[:], gw1[:], ALU.mult).then_inc(f["gw"].sem, 1)
                e.wait_ge(f["gw"].sem, f["gw"](n, 3))
                e.wait_ge(f["dv"].sem, f["dv"](n, 2))
                for i, (part, weight) in enumerate(((ew_a, gw1), (ew_b, gw2))):
                    e.tensor_tensor(part[:], iota[:].unsqueeze(1).broadcast_to([P, CT, E]), tif[:, :, i:i + 1].broadcast_to([P, CT, E]),
                                    ALU.is_equal).then_inc(f["ewab"].sem, 1)
                for i, (part, weight) in enumerate(((ew_a, gw1), (ew_b, gw2))):
                    e.wait_ge(f["ewab"].sem, f["ewab"](n, i + 1))
                    e.tensor_tensor(part[:], part[:], weight[:].unsqueeze(2).broadcast_to([P, CT, E]), ALU.mult).then_inc(f["ewab"].sem, 1)
                e.wait_ge(f["ewab"].sem, f["ewab"](n, 4))
                e.tensor_tensor(ewn[:], ew_a[:], ew_b[:], ALU.add).then_inc(f["ewn"].sem, 1)

            @staticmethod
            def experts(e, n, c):
                for piece in range(PIECES):
                    DveFfn.piece(e, n, piece, True)

        class DveRet:
            @staticmethod
            def stats(e, c):
                first = isinstance(c, int) and c == 0
                e.wait_ge(f["x_done"].sem, 1 if first else NCH)
                norm_stats(e, c, lambda t: x_flat[:, bass.ds((c * CT + t) * D, D)], st, mv, r["stat"])

            @staticmethod
            def rows(e, c):
                e.wait_ge(r["stat"].sem, r["stat"](c, 8))
                e.wait_ge(r["rstd"].sem, r["rstd"](c, 1))
                for t in range(CT):
                    e.tensor_scalar(z[:, t, :], x_flat[:, bass.ds((c * CT + t) * D, D)], mv[:, t, 0:1], r1[:, t:t + 1],
                                    ALU.subtract, ALU.mult).then_inc(r["z"].sem, 1)

            @staticmethod
            def piece(e, s, c, bb, p, base=6):
                bank = ps[:, base + p % 2, :]
                if p == 0:
                    e.wait_ge(ld["r"], 16 * NLD_R)
                if p == 1:
                    e.wait_ge(r["zT"].sem, r["zT"](s, 1))
                    e.wait_ge(r["zh"].sem, r["zh"](s, 1))
                    e.tensor_tensor(zl[:], zT[:], zh[:].bitcast(F32), ALU.subtract).then_inc(r["zl"].sem, 1)
                if p in SIN:
                    b, i = divmod(SIN.index(p), 2)
                    part = swap[:, b, 2 * i:2 * i + 2, :]
                    e.wait_ge(swapped[b].sem, swapped[b](s, 64))
                    e.tensor_tensor(part, part, sin[:].unsqueeze(1).broadcast_to([P, 2, SEQ]), ALU.mult).then_inc(r["swap_sin"].sem, 1)
                if p in ADD:
                    b, i = divmod(ADD.index(p), 2)
                    part = qkr[b][:, bb, 2 * i:2 * i + 2, :]
                    e.wait_ge(r["swap_sin"].sem, r["swap_sin"](s, 2 * b + i + 1))
                    e.wait_ge(r["cos"].sem, r["cos"](s, 2 * b + i + 1))
                    e.tensor_tensor(part, part, swap[:, b, 2 * i:2 * i + 2, :], ALU.add).then_inc(r["rot"].sem, 1)
                if p in SILU:
                    i = SILU.index(p)
                    bank = ps[:, base + (5 + i) % 2, :]
                    wait_earlier(e, r["yT"], s - 2, 2 * i + 2)
                    e.wait_ge(r["th"].sem, r["th"](s, i + 1))
                    e.scalar_tensor_tensor(sgT[bb][:, 2 * i:2 * i + 2, :], th[:, i % 2, :].rearrange("p (h t) -> p h t", h=2), 1.0,
                                           bank.rearrange("p (h t) -> p h t", h=2), ALU.add, ALU.mult).then_inc(r["sgT"].sem, 1)
                if p == OUT[1]:
                    e.wait_ge(r["wop"].sem, r["wop"](s, 1))
                    xs = x_flat[:, bass.ds(s * (SEQ // P * D), SEQ // P * D)]
                    e.scalar_tensor_tensor(xs, ps[:, 5, 0:SEQ // P * D], 0.5, xs, ALU.mult, ALU.add).then_inc(r["x_done"].sem, 1)

            @staticmethod
            def steps(e, c, steps, before, after):
                def decayed(u):
                    e.wait_ge(r["scp"].sem, r["scp"](2 * c, u + 1))
                    wait_earlier(e, r["op"], 2 * c, u - 1)
                    e.tensor_tensor(sc[:, u % 2, :], ps[:, u % 2, 0:3 * P], decay[:, u % HR, :], ALU.mult).then_inc(r["sc"].sem, 1)

                def group_stats(u):
                    b = u % 2
                    e.wait_ge(r["op"].sem, r["op"](2 * c, u + 1))
                    wait_earlier(e, r["shift"], 2 * c, u - 1)
                    for q in range(2):
                        e.bn_stats(ost[:, b, q, :], ps[:, 2 + b, q * P:(q + 1) * P]).then_inc(r["ost"].sem, 1)
                    for q in range(2):
                        e.wait_ge(r["ost"].sem, r["ost"](2 * c, 2 * u + q + 1))
                        e.sem_inc(passed)
                        e.bn_aggr(omv[:, b, q, :], ost[:, b, q, :]).then_inc(r["omv"].sem, 1)

                def group_shift(u):
                    b = u % 2
                    e.wait_ge(r["ors"].sem, r["ors"](2 * c, u + 1))
                    e.scalar_tensor_tensor(ors[:, b, 2, :], omv[:, b, :, 0], -1.0, ors[:, b, 1, :], ALU.mult, ALU.mult).then_inc(r["shift"].sem, 1)

                for u in steps:
                    if on_way(u, before):
                        decayed(u)
                    planned(e, DveRet, c, u, 0, before, after)
                    if on_way(u - 2, before):
                        group_shift(u - 2)
                    if on_way(u - 1, before):
                        group_stats(u - 1)
                    planned(e, DveRet, c, u, 1, before, after)
                    if u == 2 and after:
                        DveRet.stats(e, c + 1)
                    if u == 4 and after:
                        DveRet.rows(e, c + 1)
                    if u == 2 and not after:
                        e.wait_ge(r["x_done"].sem, CB)
                        DveFfn.stats(e, NCH, 0)
                    if u == 5 and not after:
                        DveFfn.rows(e, NCH, 0)

        @block.vector
        def _(e):
            e.wait_ge(ld["x0"], 16)
            run(e, DveFfn, DveRet)

        class ActFfn:
            @staticmethod
            def pre(e, n, c):
                pass

            @staticmethod
            def evac_out(e, n, s):
                e.wait_ge(f["pv"].sem, f["pv"](n, 2 * s + 2))
                if s >= 2:
                    e.wait_ge(f["oqp"].sem, f["oqp"](n, s - 1))
                e.activation(ou[:, s % 2, :], ps[:, 4, 0:SEQ], ACT.Identity).then_inc(f["ou"].sem, 1)

            @staticmethod
            def hidden(e, n, piece, alone=False):
                x, k = divmod(piece, 4)
                if x == E:
                    return
                e.wait_ge(f["zps"].sem, f["zps"](n, piece + 1))
                if k == 0 and x >= 2:
                    e.wait_ge(f["outp"].sem, f["outp"](n, x - 1))
                e.activation(hid[:, x % 2, k, :], ps[:, hidden_bank(piece, alone), :], ACT.Relu, bias=vec[:, B1 + piece:B1 + piece + 1]).then_inc(f["hid"].sem, 1)

            @staticmethod
            def steps(e, n, c, moe, ahead):
                fill = filler(0, moe, lambda piece: ActFfn.hidden(e, n - 1, piece))

                def grown(u):
                    e.wait_ge(f["st_ps"].sem, f["st_ps"](n, u + 1))
                    if u >= 2:
                        e.wait_ge(f["pv"].sem, f["pv"](n, u - 1))
                    e.activation(pt[:, u % 2, :, :], ps[:, 2:4, :], ACT.Exp, scale=float(DK) ** -0.5).then_inc(f["pexp"].sem, 1)

                fill(START - 1)
                if moe:
                    ActFfn.weights_t(e, n - 1)
                fill(1)
                for s in range(8):
                    fill(1)
                    grown(2 * s)
                    if s:
                        ActFfn.evac_out(e, n, s - 1)
                    fill(1)
                    grown(2 * s + 1)
                    fill(FILL - 2)
                    if not moe and n == 0:
                        e.wait_ge(ld["moe"], 16 * NLD_MOE)
                        e.activation(w1h[:, s, :], w1_in[:, s * FT * P:(s + 1) * FT * P], ACT.Identity).then_inc(w1_high.sem, 1)
                        e.activation(rwh[:, 2 * s:2 * s + 2, :], rw_in[:, 2 * s:2 * s + 2, :], ACT.Identity).then_inc(rw_high.sem, 1)
                ActFfn.evac_out(e, n, 7)

            @staticmethod
            def turn(e, n, c, tail, head, moe):
                fill = filler(REST, moe, lambda piece: ActFfn.hidden(e, n - 1, piece))

                def query_key(*groups):
                    for i in groups if head else ():
                        e.wait_ge(f["qkp"].sem, f["qkp"](n + 1, i + 1))
                        if i >= 2:
                            e.wait_ge(f["pack"].sem, f["pack"](n + 1, i - 1))
                        e.activation(hi[:, i % 2, :], ps[:, i % 4, :], ACT.Identity, bias=bqk[:, i % 2, i // 2:i // 2 + 1]).then_inc(f["hi"].sem, 1)
                        e.activation(tqk[:, i % 2, :], ps[:, i % 4, :], ACT.Identity, scale=mask[:, 0, i % 2:i % 2 + 1], bias=bql[:, i % 2, i // 2:i // 2 + 1]).then_inc(f["tqk"].sem, 1)

                if not tail:
                    e.wait_ge(ld["w"], 16 * NLD_W)
                if head:
                    e.wait_ge(f["hTp"].sem, f["hTp"](n + 1, 1))
                    e.activation(hT[:], ps[:, 3, :], ACT.Identity, scale=vec[:, G1:G1 + 1], bias=vec[:, L1B:L1B + 1]).then_inc(f["hT"].sem, 1)
                fill(1)
                if tail:
                    e.wait_ge(f["oTp"].sem, f["oTp"](n, 1))
                    e.activation(oT[:], ps[:, 5, :], ACT.Identity).then_inc(f["oT"].sem, 1)
                query_key(0, 1)
                fill(1)
                query_key(2)
                fill(1)
                query_key(3)
                fill(1)
                if tail:
                    e.wait_ge(f["h2Tp"].sem, f["h2Tp"](n, 1))
                    e.activation(h2n[:], ps[:, 5, :], ACT.Identity, scale=vec[:, G2:G2 + 1], bias=vec[:, L2B:L2B + 1]).then_inc(f["h2n"].sem, 1)
                query_key(4, 5)
                fill(1)
                if tail:
                    e.wait_ge(f["h2n"].sem, f["h2n"](n, 1))
                    e.activation(h2h[:], h2n[:], ACT.Identity).then_inc(f["h2h"].sem, 1)
                query_key(6, 7)
                if tail:
                    e.wait_ge(f["dv"].sem, f["dv"](n, 1))
                    e.activation(ev[:], dv[:], ACT.Exp).then_inc(f["ev"].sem, 1)
                if not head:
                    ActFfn.weights_t(e, n)

            @staticmethod
            def weights_t(e, n):
                e.wait_ge(f["ewTp"].sem, f["ewTp"](n, 1))
                e.activation(ewT[:], ps[0:E, 5, :], ACT.Identity).then_inc(f["ewT"].sem, 1)

            @staticmethod
            def experts(e, n, c):
                for piece in range(PIECES):
                    ActFfn.hidden(e, n, piece, True)

        class ActRet:
            @staticmethod
            def piece(e, s, c, bb, p, base=6):
                bank = ps[:, base + p % 2, :]
                if p == 0:
                    e.wait_ge(r["zTp"].sem, r["zTp"](s, 1))
                    e.activation(zT[:], ps[:, 5, 0:SEQ], ACT.Identity).then_inc(r["zT"].sem, 1)
                    e.activation(zh[:], ps[:, 5, 0:SEQ], ACT.Identity).then_inc(r["zh"].sem, 1)
                if 1 <= p <= 4:
                    b, i = divmod(p - 1, 2)
                    e.wait_ge(r["qkp"].sem, r["qkp"](s, p))
                    e.activation(qkr[b][:, bb, 2 * i:2 * i + 2, :], bank.rearrange("p (h t) -> p h t", h=2), ACT.Identity).then_inc(r["qk"].sem, 1)
                if 9 <= p <= 12:
                    i = p - 9
                    e.wait_ge(r["vp"].sem, r["vp"](s, i + 1))
                    e.activation(vr[:, bb, i // 2, (i % 2) * 512:(i % 2 + 1) * 512], bank, ACT.Identity).then_inc(r["vr"].sem, 1)
                if 5 <= p <= 8:
                    i = p - 5
                    e.wait_ge(r["gp"].sem, r["gp"](s, i + 1))
                    wait_earlier(e, r["sgT"], s, i - 1)
                    e.activation(th[:, i % 2, :], bank, ACT.Tanh, scale=0.5).then_inc(r["th"].sem, 1)

            @staticmethod
            def steps(e, c, steps, before, after):
                def normed(u):
                    b = u % 2
                    e.wait_ge(r["shift"].sem, r["shift"](2 * c, u + 1))
                    wait_earlier(e, r["ohTp"], 2 * c, u - 1)
                    for q in range(2):
                        e.activation(oh[:, b, q, :], ps[:, 2 + b, q * P:(q + 1) * P], ACT.Identity, scale=ors[:, b, 1, q:q + 1],
                                     bias=ors[:, b, 2, q:q + 1]).then_inc(r["oh"].sem, 1)

                def affine(u):
                    h = u % HR
                    e.wait_ge(r["ohTp"].sem, r["ohTp"](2 * c, u + 1))
                    wait_earlier(e, r["yT"], 2 * c, u - 1)
                    e.activation(on[:, u % 2, :], ps[:, 4, 0:SEQ], ACT.Identity, scale=vec[:, GNW + h:GNW + h + 1],
                                 bias=vec[:, GNB + h:GNB + h + 1]).then_inc(r["on"].sem, 1)

                for u in steps:
                    planned(e, ActRet, c, u, 0, before, after)
                    if on_way(u - 2, before):
                        normed(u - 2)
                    if on_way(u - 3, before):
                        affine(u - 3)
                    planned(e, ActRet, c, u, 1, before, after)

        @block.scalar
        def _(e):
            e.wait_ge(zeroed.sem, 1)
            e.activation(ev[:], mhalf[:], ACT.Exp)
            run(e, ActFfn, ActRet)

        def transposes(e, dst, src, sig):
            for t in range(CT):
                last = e.transpose(dst(t), src(t), ident[:])
            last.then_inc(sig.sem, 1)

        class PeFfn:
            @staticmethod
            def pre(e, n, c):
                pass

            @staticmethod
            def query_key(e, n, i):
                if i >= 4:
                    e.wait_ge(f["tqk"].sem, f["tqk"](n, i - 3))
                wp = (wkp if i % 2 else wqp)[:, i // 2, :, :, :].rearrange("p j a k -> p (j a k)")
                e.matmul(ps[:, i % 4, :], wp, hT[:], start=True, stop=True).then_inc(f["qkp"].sem, 1)

            @staticmethod
            def value_rows(e, n, bank):
                for t in range(CT):
                    last = e.matmul(ps[:, bank, t * D:(t + 1) * D], hT[:, t * P:(t + 1) * P], wv[:], start=True, stop=True)
                last.then_inc(f["vps"].sem, 1)

            @staticmethod
            def scores(e, n, s, pr, moe):
                bb, g = divmod(s, GA)
                lo = bb * SEQ
                u = 2 * s + pr
                if u == 0 and moe:
                    e.wait_ge(f["pack"].sem, f["pack"](n, 8))
                elif s < GA and pr == 0 and not moe:
                    e.wait_ge(f["pack"].sem, f["pack"](n, 2 * s + 2))
                if u == 2 and not moe:
                    e.wait_ge(f["tqk"].sem, f["tqk"](n, 6))
                if u:
                    e.wait_ge(f["smax"].sem, f["smax"](n, u if moe or u == 1 else u - 1))
                bank = ps[:, score_banks(u, moe), :]
                for q in range(2):
                    for jj in range(2):
                        j = 32 * (2 * pr + jj)
                        last = e.matmul(bank[:, jj, q * SEQ:(q + 1) * SEQ], qp[j:j + 32, g, lo + q * P:lo + (q + 1) * P],
                                        kp[j:j + 32, g, lo:lo + SEQ], start=True, stop=True)
                last.then_inc(f["s_ps"].sem, 1)

            @staticmethod
            def scores_t(e, n, s, pr):
                bb, g = divmod(s, GA)
                lo = bb * SEQ
                u = 2 * s + pr
                if u:
                    e.wait_ge(f["pexp"].sem, f["pexp"](n, u))
                else:
                    e.wait_ge(f["tqk"].sem, f["tqk"](n, 8))
                if pr == 0:
                    e.wait_ge(f["qm"].sem, f["qm"](n, s + 1))
                for q in range(2):
                    for jj in range(2):
                        j = 32 * (2 * pr + jj)
                        last = e.matmul(ps[:, 2 + jj, q * SEQ:(q + 1) * SEQ], kp[j:j + 32, g, lo + q * P:lo + (q + 1) * P],
                                        qm[j:j + 32, s % 2, :], start=True, stop=True)
                last.then_inc(f["st_ps"].sem, 1)

            @staticmethod
            def values(e, n, s, pr):
                bb, g = divmod(s, GA)
                u = 2 * s + pr
                if u == 0:
                    e.wait_ge(f["vaug"].sem, f["vaug"](n, 1))
                e.wait_ge(f["pexp"].sem, f["pexp"](n, u + 1))
                if pr == 0 and s:
                    e.wait_ge(f["ou"].sem, f["ou"](n, s))
                for jj in range(2):
                    j = 2 * pr + jj
                    for k in range(2):
                        last = e.matmul(ps[32 * j:32 * j + 32, 4, 0:SEQ], vaug[:, 2 * bb + k, 4 * g + j, :], pt[:, u % 2, jj, k * SEQ:(k + 1) * SEQ],
                                        start=(k == 0), stop=(k == 1), tile_position=(0, 32 * j))
                last.then_inc(f["pv"].sem, 1)

            @staticmethod
            def out_t(e, n, s):
                e.wait_ge(f["ou"].sem, f["ou"](n, s + 1))
                if s == 7:
                    e.wait_ge(f["o_tm"].sem, f["o_tm"](n, 7))
                for q in range(2):
                    last = e.transpose(ps[:, 5, q * P:(q + 1) * P], ou[:, s % 2, q * P:(q + 1) * P], ident[:])
                last.then_inc(f["oqp"].sem, 1)

            @staticmethod
            def keep_clock(e, bank, many):
                for _ in range(many):
                    e.matmul(ps[:, bank, SEQ:2 * SEQ], kp[:, 0, 0:P], qp[:, 0, 0:SEQ], start=True, stop=True)

            @staticmethod
            def expert_piece(e, n, piece, alone=False):
                x, k = divmod(piece, 4)
                if x < E:
                    if piece == 0:
                        e.wait_ge(f["h2l"].sem, f["h2l"](n, 1))
                        e.wait_ge(w1_low.sem, E)
                    held = 2 if alone else 1
                    if piece >= held:
                        e.wait_ge(f["hid"].sem, f["hid"](n, piece + 1 - held))
                    parts = ((w1h, h2h), (w1l, h2h), (w1h, h2l))
                    for i, (w, h) in enumerate(parts):
                        last = e.matmul(ps[:, hidden_bank(piece, alone), :], w[:, x, k * P:(k + 1) * P], h[:], start=(i == 0), stop=(i == 2))
                    last.then_inc(f["zps"].sem, 1)
                if x:
                    if k == 0:
                        e.wait_ge(f["hid"].sem, f["hid"](n, FT * x))
                        if x >= (3 if alone else 2):
                            e.wait_ge(f["tmp"].sem, f["tmp"](n, x - 2 if alone else x - 1))
                        else:
                            e.wait_ge(f["ew"].sem, f["ew"](n, 1))
                    for i in range(FT):
                        last = e.matmul(ps[:, out_bank(x - 1, alone), k * D:(k + 1) * D], hid[:, (x - 1) % 2, i, k * P:(k + 1) * P], w2[:, x - 1, i, :],
                                        start=(i == 0), stop=(i == FT - 1))
                    if k == 3:
                        last.then_inc(f["outp"].sem, 1)

            @staticmethod
            def steps(e, n, c, moe, ahead):
                fill = filler(0, moe, lambda piece: PeFfn.expert_piece(e, n - 1, piece))
                if not moe:
                    PeFfn.scores(e, n, 0, 0, moe)
                fill(START - 3)
                if not moe:
                    PeFfn.query_key(e, n, 4)
                    PeFfn.query_key(e, n, 5)
                PeFfn.scores(e, n, 0, 1, moe)
                fill(2)
                if moe:
                    PeFfn.weights_t(e, n - 1)
                fill(1)
                if moe:
                    PeFfn.bias(e, n - 1)
                if not moe:
                    PeFfn.query_key(e, n, 6)
                    PeFfn.query_key(e, n, 7)
                for s in range(8):
                    e.wait_ge(f["smax"].sem, f["smax"](n, 2 * s + 2))
                    if s >= 2:
                        e.wait_ge(f["o_tm"].sem, f["o_tm"](n, s - 1))
                    for q in range(2):
                        last = e.transpose(ps[:, 5, q * P:(q + 1) * P], msp[:, s % 2, q, :], ident[:])
                    last.then_inc(f["mTp"].sem, 1)
                    if s < 7:
                        PeFfn.scores(e, n, s + 1, 0, moe)
                    fill(1)
                    if s == 0 and not moe:
                        PeFfn.value_rows(e, n, 4)
                    if s and not moe:
                        PeFfn.keep_clock(e, 4, 6)
                    PeFfn.scores_t(e, n, s, 0)
                    if s:
                        PeFfn.values(e, n, s - 1, 1)
                    if s < 7:
                        PeFfn.scores(e, n, s + 1, 1, moe)
                    fill(1)
                    if not moe:
                        PeFfn.keep_clock(e, 5, 4)
                    PeFfn.scores_t(e, n, s, 1)
                    fill(FILL - 3)
                    if s:
                        PeFfn.out_t(e, n, s - 1)
                    PeFfn.values(e, n, s, 0)
                    fill(1)
                PeFfn.values(e, n, 7, 1)

            @staticmethod
            def turn(e, n, c, tail, head, moe):
                fill = filler(REST, moe, lambda piece: PeFfn.expert_piece(e, n - 1, piece))

                def query_key(*groups):
                    for i in groups if head else ():
                        if i == 2 and tail:
                            e.wait_ge(f["vaug"].sem, f["vaug"](n + 1, 1))
                        PeFfn.query_key(e, n + 1, i)

                if not tail:
                    e.wait_ge(ld["w"], 16 * NLD_W)
                if head:
                    e.wait_ge(f["z"].sem, f["z"](n + 1, 4))
                    transposes(e, lambda t: ps[:, 3, t * P:(t + 1) * P], lambda t: z[:, t, :], f["hTp"])
                fill(1)
                if tail:
                    PeFfn.out_t(e, n, 7)
                if head:
                    e.wait_ge(f["hT"].sem, f["hT"](n + 1, 1))
                if head and tail:
                    PeFfn.value_rows(e, n + 1, 2)
                if tail:
                    e.wait_ge(f["o_tm"].sem, f["o_tm"](n, 8))
                    transposes(e, lambda t: ps[:, 5, t * P:(t + 1) * P], lambda t: o_tm[:, t, :], f["oTp"])
                query_key(0)
                if tail:
                    e.wait_ge(ld["late"], 16 * NLD_LATE)
                    e.wait_ge(f["oT"].sem, f["oT"](n, 1))
                    for t in range(CT):
                        last = e.matmul(ps[:, 4, t * D:(t + 1) * D], oT[:, t * P:(t + 1) * P], wo[:], start=True, stop=True)
                    last.then_inc(f["x1p"].sem, 1)
                query_key(1)
                fill(1)
                query_key(2)
                fill(1)
                query_key(3)
                if not tail:
                    return
                fill(1)
                if not moe:
                    query_key(4, 5)
                if tail:
                    e.wait_ge(f["z2"].sem, f["z2"](n, 4))
                    transposes(e, lambda t: ps[:, 5, t * P:(t + 1) * P], lambda t: o_tm[:, t, :], f["h2Tp"])
                if moe:
                    query_key(4, 5)
                if tail:
                    e.wait_ge(f["h2n"].sem, f["h2n"](n, 1))
                    for t in range(CT):
                        last = e.matmul(ps[:, 4, t * E:(t + 1) * E], h2n[:, t * P:(t + 1) * P], gate_w[:], start=True, stop=True)
                    last.then_inc(f["lgp"].sem, 1)
                query_key(6)
                fill(1)
                query_key(7)
                fill(1)
                if not head:
                    PeFfn.weights_t(e, n)
                fill(1)
                if head:
                    PeFfn.scores(e, n + 1, 0, 0, True)
                fill(PIECES - REST - 7)
                if not head:
                    PeFfn.bias(e, n)

            @staticmethod
            def weights_t(e, n):
                e.wait_ge(f["ewn"].sem, f["ewn"](n, 1))
                for t in range(CT):
                    last = e.transpose(ps[0:E, 5, t * P:(t + 1) * P], ewn[:, t, :], ident[:])
                last.then_inc(f["ewTp"].sem, 1)

            @staticmethod
            def bias(e, n):
                e.wait_ge(f["ewT"].sem, f["ewT"](n, 1))
                for t in range(CT):
                    last = e.matmul(ps[:, 4, t * D:(t + 1) * D], ewT[:, t * P:(t + 1) * P], b2[:], start=True, stop=True)
                last.then_inc(f["b2p"].sem, 1)

            @staticmethod
            def experts(e, n, c):
                for piece in range(PIECES):
                    PeFfn.expert_piece(e, n, piece, True)

        class PeRet:
            @staticmethod
            def released(e, s, p):
                if p <= 4:
                    e.wait_ge(r["qk"].sem, r["qk"](s, p))
                elif p <= 8:
                    e.wait_ge(r["sgT"].sem, r["sgT"](s, p - 4))
                else:
                    e.wait_ge(r["vr"].sem, r["vr"](s, p - 8))

            @staticmethod
            def piece(e, s, c, bb, p, base=6):
                if p in OUT:
                    t = p - OUT[0]
                    e.wait_ge(r["yT"].sem, r["yT"](s, 8))
                    wait_earlier(e, r["x_done"], s, 0)
                    for h in range(HR):
                        last = e.matmul(ps[:, 5, t * D:(t + 1) * D], yT[:, bb, h, t * P:(t + 1) * P], rwo[:, h, :], start=(h == 0), stop=(h == HR - 1))
                    if t == 1:
                        last.then_inc(r["wop"].sem, 1)
                    return
                if p >= PROJ:
                    return
                bank = ps[:, base + p % 2, :]
                if p >= 3:
                    PeRet.released(e, s, p - 2)
                elif p and not (isinstance(s, int) and s == 0):
                    PeRet.released(e, s - 1, p + PROJ - 3)
                    if isinstance(s, int) and s == 1:
                        e.wait_ge(f["tmp"].sem, NCH * E)
                if p == 0:
                    e.wait_ge(ld["r"], 16 * NLD_R)
                    e.wait_ge(r["z"].sem, r["z"](c, 4))
                    wait_earlier(e, r["x_done"], s, -2)
                    for t in range(2):
                        last = e.transpose(ps[:, 5, t * P:(t + 1) * P], z[:, 2 * bb + t, :], ident[:])
                    last.then_inc(r["zTp"].sem, 1)
                elif p <= 4:
                    if p == 1:
                        e.wait_ge(r["zT"].sem, r["zT"](s, 1))
                    for k in range(2):
                        last = e.matmul(bank[:, k * SEQ:(k + 1) * SEQ], rw[:, 2 * (p - 1) + k, :], zT[:], start=True, stop=True)
                    last.then_inc(r["qkp"].sem, 1)
                elif p <= 8:
                    if p == 5:
                        e.wait_ge(r["zl"].sem, r["zl"](s, 1))
                        e.wait_ge(rw_low.sem, 8)
                    for k in range(2):
                        for i, (w, x) in enumerate(((rwh, zh), (rwl, zh), (rwh, zl))):
                            last = e.matmul(bank[:, k * SEQ:(k + 1) * SEQ], w[:, 8 + 2 * (p - 5) + k, :], x[:], start=(i == 0), stop=(i == 2))
                    last.then_inc(r["gp"].sem, 1)
                else:
                    t, half = divmod(p - 9, 2)
                    for i, (w, x) in enumerate(((rwh, zh), (rwl, zh), (rwh, zl))):
                        last = e.matmul(bank, x[:, t * P:(t + 1) * P], w[:, 4 * half:4 * half + 4, :].rearrange("p k o -> p (k o)"),
                                        start=(i == 0), stop=(i == 2))
                    last.then_inc(r["vp"].sem, 1)

            @staticmethod
            def steps(e, c, steps, before, after):
                def scores(u):
                    h, bb = u % HR, u // HR % 2
                    j, hp = 64 * (h % 2), h // 2
                    if h == 0:
                        e.wait_ge(r["rot"].sem, r["rot"](2 * c, 4 * (u // HR) + 4))
                    wait_earlier(e, r["sc"], 2 * c, u - 1)
                    e.matmul(ps[:, u % 2, 0:SEQ], qkr[1][j:j + DR, bb, hp, 0:P], qkr[0][j:j + DR, bb, hp, :], start=True, stop=True)
                    e.matmul(ps[:, u % 2, SEQ:SEQ + P], qkr[1][j:j + DR, bb, hp, P:SEQ], qkr[0][j:j + DR, bb, hp, P:SEQ],
                             start=True, stop=True).then_inc(r["scp"].sem, 1)

                def values(u):
                    h, bb, b = u % HR, u // HR % 2, u % 2
                    e.wait_ge(r["sc"].sem, r["sc"](2 * c, u + 1))
                    if h == 0:
                        e.wait_ge(r["vr"].sem, r["vr"](2 * c, 4 * (u // HR) + 4))
                    wait_earlier(e, r["oh"], 2 * c, 2 * u - 2)
                    v = [vr[:, bb, k, h * P:(h + 1) * P] for k in range(2)]
                    e.matmul(ps[:, 2 + b, 0:P], sc[:, b, 0:P], v[0], start=True, stop=True)
                    e.matmul(ps[:, 2 + b, P:2 * P], sc[:, b, P:2 * P], v[0], start=True, stop=False)
                    e.matmul(ps[:, 2 + b, P:2 * P], sc[:, b, 2 * P:3 * P], v[1], start=False, stop=True).then_inc(r["op"].sem, 1)

                def normed_t(u):
                    e.wait_ge(r["oh"].sem, r["oh"](2 * c, 2 * u + 2))
                    wait_earlier(e, r["on"], 2 * c, u)
                    for q in range(2):
                        last = e.transpose(ps[:, 4, q * P:(q + 1) * P], oh[:, u % 2, q, :], ident[:])
                    last.then_inc(r["ohTp"].sem, 1)

                for u in steps:
                    if on_way(u, before):
                        scores(u)
                    planned(e, PeRet, c, u, 0, before, after)
                    if on_way(u - 1, before):
                        values(u - 1)
                    if on_way(u - 3, before):
                        normed_t(u - 3)
                    planned(e, PeRet, c, u, 1, before, after)

        @block.tensor
        def _(e):
            run(e, PeFfn, PeRet)


def kernel(**inputs):
    import concourse.bacc as bacc
    from concourse.bass_utils import run_bass_kernel_spmd as run

    x = np.asarray(inputs["L0_attn_x"])
    nc = bacc.Bacc("TRN2", target_bir_lowering=False, num_devices=1)
    arrays, aps = {}, {}
    for name, v in {**inputs, **laid_out({k: np.asarray(v) for k, v in inputs.items()}), **constants(x.shape[0] * x.shape[1] // P)}.items():
        v = np.ascontiguousarray(v)
        arrays["in_" + name] = v
        aps[name] = nc.dram_tensor("in_" + name, v.shape, mybir.dt.from_np(v.dtype), kind="ExternalInput").ap()
    out = nc.dram_tensor("out_x", x.shape, F32, kind="ExternalOutput").ap()
    build(nc, aps, out)
    return run(nc, [arrays], core_ids=[0]).results[0]["out_x"]
```
